# Optimizing a Trainium2 kernel written in Bass

```python
import numpy as np
import jax
import jax.numpy as jnp

def _softmax(x, axis=-1):
    return jax.nn.softmax(x, axis=axis)

def _gelu(x):
    return jax.nn.gelu(x, approximate=True)

def _silu(x):
    return jax.nn.silu(x)

def _sigmoid(x):
    return jax.nn.sigmoid(x)

def _layernorm(x, axis=-1, eps=1e-05):
    m = jnp.mean(x, axis=axis, keepdims=True)
    v = jnp.var(x, axis=axis, keepdims=True)
    return (x - m) / jnp.sqrt(v + eps)

def _scatter_add(tgt, idx, src, axis=0):
    return tgt.at[idx].add(src)

def _segment_sum(src, seg, n):
    return jax.ops.segment_sum(src, seg, n)
kernel_name = 'mk_prb_d1_jaxref_r8_73d949'

def setup_inputs(seed: int=0):
    np.random.seed(seed)
    _w = jnp.asarray

    def _L0_attn_setup():
        import jax, jax.numpy as jnp
        import numpy as np
        from math import sqrt
        ROPE_BASE = 6000.0

        def _rope_tables(seq_len, rope_dim, dtype):
            inv_freq = 1.0 / ROPE_BASE ** (jnp.arange(0, rope_dim, 2, dtype=jnp.float32) / rope_dim)
            t = jnp.arange(seq_len, dtype=jnp.float32)
            freqs = jnp.outer(t, inv_freq)
            emb = jnp.concatenate([freqs, freqs], axis=-1)
            return (jnp.cos(emb).astype(dtype), jnp.sin(emb).astype(dtype))

        def _rotate_half(x):
            x1, x2 = jnp.split(x, 2, axis=-1)
            return jnp.concatenate([-x2, x1], axis=-1)
        key = jax.random.key(seed)
        k1, k2, k3 = jax.random.split(key, 3)
        B, S, D = (2, 256, 128)
        H, DK = (16, 64)
        x = jax.random.normal(k1, (B, S, D), dtype=jnp.float32)
        W_qkv = jax.random.normal(k2, (3, H, DK, D), dtype=jnp.float32) * 0.02
        W_o = jax.random.normal(k3, (D, H * DK), dtype=jnp.float32) * 0.02
        return {'x': x, 'W_qkv': W_qkv, 'W_o': W_o}
    _L0_attn_in = _L0_attn_setup()

    def _L0_ffn_setup():
        import jax, jax.numpy as jnp
        import numpy as np
        TOP_K = 2
        key = jax.random.key(seed)
        ks = jax.random.split(key, 5)
        B, T, D, F, E = (2, 256, 128, 512, 8)
        x = jax.random.normal(ks[0], (B, T, D), dtype=jnp.float32)
        router_w = jax.random.normal(ks[1], (D, E + 1), dtype=jnp.float32) * 0.02
        router_b = jax.random.normal(ks[2], (E + 1,), dtype=jnp.float32) * 0.02
        w1 = jax.random.normal(ks[3], (E, D, F), dtype=jnp.float32) * 0.02
        w2 = jax.random.normal(ks[4], (E, F, D), dtype=jnp.float32) * 0.02
        return {'x': x, 'router_w': router_w, 'router_b': router_b, 'w1': w1, 'w2': w2}
    _L0_ffn_in = _L0_ffn_setup()
    _d = {'L0_attn_x': _L0_attn_in['x'], 'L0_attn_W_qkv': _L0_attn_in['W_qkv'], 'L0_attn_W_o': _L0_attn_in['W_o'], 'L0_ffn_router_w': _L0_ffn_in['router_w'], 'L0_ffn_router_b': _L0_ffn_in['router_b'], 'L0_ffn_w1': _L0_ffn_in['w1'], 'L0_ffn_w2': _L0_ffn_in['w2']}
    _x0 = _d['L0_attn_x']
    _d['L0_attn_x'] = jax.random.normal(jax.random.fold_in(jax.random.key(seed), 1), (32, 256, 128), dtype=_x0.dtype)
    del _x0
    return _d

def reference(L0_attn_x, L0_attn_W_qkv, L0_attn_W_o, L0_ffn_router_w, L0_ffn_router_b, L0_ffn_w1, L0_ffn_w2):

    def _L0_attn_ref(x, W_qkv, W_o):
        import jax, jax.numpy as jnp
        import numpy as np
        from math import sqrt
        ROPE_BASE = 6000.0

        def _rope_tables(seq_len, rope_dim, dtype):
            inv_freq = 1.0 / ROPE_BASE ** (jnp.arange(0, rope_dim, 2, dtype=jnp.float32) / rope_dim)
            t = jnp.arange(seq_len, dtype=jnp.float32)
            freqs = jnp.outer(t, inv_freq)
            emb = jnp.concatenate([freqs, freqs], axis=-1)
            return (jnp.cos(emb).astype(dtype), jnp.sin(emb).astype(dtype))

        def _rotate_half(x):
            x1, x2 = jnp.split(x, 2, axis=-1)
            return jnp.concatenate([-x2, x1], axis=-1)
        B, S, D = x.shape
        _, H, DK, _ = W_qkv.shape
        rope_dim = DK // 2
        qkv = jnp.einsum('bsm,qhdm->bqhsd', x, W_qkv)
        cos, sin = _rope_tables(S, rope_dim, x.dtype)
        qk = qkv[:, :2, :, :, :rope_dim]
        qk_rot = qk * cos + _rotate_half(qk) * sin
        qkv = qkv.at[:, :2, :, :, :rope_dim].set(qk_rot)
        Q, K, V = (qkv[:, 0], qkv[:, 1], qkv[:, 2])
        scores = jnp.einsum('bhqd,bhkd->bhqk', Q, K)
        causal = jnp.triu(jnp.ones((S, S), dtype=bool), k=1)
        scores = jnp.where(causal, -jnp.inf, scores) / sqrt(DK)
        attn = jax.nn.softmax(scores, axis=-1)
        out = jnp.einsum('bhqk,bhkd->bhqd', attn, V)
        out = out.transpose(0, 2, 1, 3).reshape(B, S, H * DK)
        return jnp.einsum('bsh,dh->bsd', out, W_o)

    def _L0_ffn_ref(x, router_w, router_b, w1, w2):
        import jax, jax.numpy as jnp
        import numpy as np
        TOP_K = 2
        E = w1.shape[0]
        logits = x @ router_w + router_b
        probs = jax.nn.softmax(logits, axis=-1)
        top_v, top_i = jax.lax.top_k(probs, TOP_K)
        gates = jnp.sum(jax.nn.one_hot(top_i, E + 1, dtype=x.dtype) * top_v[..., None], axis=-2)
        h = jax.nn.gelu(jnp.einsum('btd,edf->ebtf', x, w1), approximate=False)
        y = jnp.einsum('ebtf,efd->ebtd', h, w2)
        out = jnp.einsum('bte,ebtd->btd', gates[..., :E], y) + gates[..., E:] * x
        return out
    x = L0_attn_x
    xn = _layernorm(x, axis=-1)
    x = x + _L0_attn_ref(xn, L0_attn_W_qkv, L0_attn_W_o) + _L0_ffn_ref(xn, L0_ffn_router_w, L0_ffn_router_b, L0_ffn_w1, L0_ffn_w2)
    return x

_drawn_inputs = setup_inputs


def setup_inputs(seed=0):
    import zlib

    import numpy as np

    out = dict(_drawn_inputs(seed))
    spreads = {}
    factors = {'L0_ffn_router_b': 4.64,
     'L0_ffn_w1': 5.693,
     'L0_ffn_w2': 5.602,
     'L0_attn_W_qkv': 2.808,
     'L0_attn_W_o': 2.831}
    for name, (base, spread) in spreads.items():
        noise = np.random.default_rng([zlib.crc32(name.encode()), seed]).standard_normal(out[name].shape)
        drawn = base * np.exp(spread * noise) if base else spread * noise
        out[name] = jnp.asarray(drawn.astype(out[name].dtype))
    for name, factor in factors.items():
        out[name] = (out[name] * factor).astype(out[name].dtype)
    return out
```

```python
from contextlib import ExitStack

import concourse.bass as bass
from concourse import mybir

F32 = mybir.dt.float32
F16 = mybir.dt.float16
ALU = mybir.AluOpType
ACT = mybir.ActivationFunctionType
AX = mybir.AxisListType

P = 128
B, SEQ, D = 32, 256, 128
H, DK = 16, 64
ROPE = DK // 2
E, F = 8, 512
NT = B * SEQ // P
TPS = SEQ // P
GRP = 4
NG = H // GRP
FB = F // P
CH = 512
NC = B * SEQ // CH
CT = CH // P
LC = 16
NL = NT // LC
LQ = LC // 4
W_SCALE = 64.0
UNSCALE = 1.0 / W_SCALE
EPS = 1e-5
MASKED = 3.0e38
PW = P + 2 * P

PROLOGUE = [("rest", 0), ("rest", 1), ("rest", 2), ("rest", 3)] + [("rope", j) for j in range(8)] + [("v_low", 0), ("v_low", 1)]
BESIDE = [
    [], [], [], [("rest", 0), ("rest", 1)],
    [("rest", 2), ("y", 0)], [("rest", 3), ("y", 1)], [("rope", 0), ("rope", 1)], [("rope", 2), ("v_high", 0)],
    [("rope", 3), ("rope", 4)], [("rope", 5), ("v_high", 1)], [("rope", 6), ("rope", 7)], [],
    [], [("v_low", 0)], [("v_low", 1)], [],
]
NEXT = ("rest", "rope", "v_low")
INV_LAG, T_LAG, PV_LAG = 2, 3, 4


def units_of(first, last):
    out = []
    for s, units in enumerate(BESIDE):
        for kind, j in units:
            if (first and kind == "y") or (last and kind in NEXT):
                continue
            out.append((s, kind, j))
    return out


FULL = len(units_of(False, False))
OPEN = len(PROLOGUE) + len(units_of(True, False))


def unit_base(b, first):
    return len(PROLOGUE) if first else OPEN + FULL * (b - 1)


def attention_and_experts(nc, x, wqk, wv, wo, rw, rb, w1, w2, tables, out):
    with ExitStack() as ctx:
        def sb(name, shape, dt):
            return ctx.enter_context(nc.sbuf_tensor(name, shape, dt))

        def sem(name):
            return ctx.enter_context(nc.semaphore(name))

        acc = sb("acc", [P, NT, D], F32)
        xnT_hi = sb("xnT_hi", [P, NT * P], F16)
        xnT_lo = sb("xnT_lo", [P, NT * P], F16)
        wqk_hi = sb("wqk_hi", [P, 24, P], F16)
        wqk_lo = sb("wqk_lo", [P, 24, P], F16)
        wv_hi = sb("wv_hi", [P, H * DK], F16)
        wv_lo = sb("wv_lo", [P, H * DK], F16)
        wo_hi = sb("wo_hi", [P, 8, D], F16)
        wo_lo = sb("wo_lo", [P, 8, D], F16)
        w1_hi = sb("w1_hi", [P, E, F], F16)
        w1_lo = sb("w1_lo", [P, E, F], F16)
        w2_hi = sb("w2_hi", [P, E, FB, D], F16)
        w2_lo = sb("w2_lo", [P, E, FB, D], F16)
        rw_f = sb("rw_f", [P, E + 1], F32)
        rw_hi = sb("rw_hi", [P, E + 1], F16)
        rw_lo = sb("rw_lo", [P, E + 1], F16)
        rb_all = sb("rb_all", [P, E + 1], F32)
        gates = sb("gates", [P, NT, E + 1], F32)
        ident = sb("ident", [P, P], F32)
        rank = sb("rank", [P, E + 1], F32)
        mean = sb("mean", [P, NT], F32)
        rstd = sb("rstd", [P, NT], F32)
        small = sb("small", [P, 4, NT], F32)
        half = sb("half", [P, NT], F32)
        arena = sb("arena", [P, 18 * 1024], F32)

        def view(at, words, dt=F32):
            v = arena[:, at:at + words]
            return v if dt == F32 else v.bitcast(dt)

        stage_a = view(0, 4096)
        stage_b = view(4096, 4096)
        xc = [view(8192 + i * 2048, 2048).rearrange("p (t d) -> p t d", d=D) for i in range(2)]
        sq = view(12288, 2048).rearrange("p (t d) -> p t d", d=D)
        route = [view(14336 + i * 576, 576).rearrange("p (t e) -> p t e", e=E + 1) for i in range(5)]
        k_stack = view(0, 2048, F16).rearrange("p (h t) -> p h t", t=SEQ)
        q_stack = view(2048, 4096, F16).rearrange("p (r l n) -> p r l n", r=GRP, l=2)
        v_sb = view(6144, 2048).rearrange("p (t n) -> p t n", t=TPS)
        q_staged = view(8192, 2048, F16).rearrange("p (k l n) -> p k l n", k=2, l=2)
        k_staged = view(10240, 2048, F16).rearrange("p (l k n) -> p l k n", k=2, l=2)
        ot_hi = view(12288, 1024, F16).rearrange("p (j t) -> p j t", j=8)
        ot_lo = view(13312, 1024, F16).rearrange("p (j t) -> p j t", j=8)
        turned = [view(14336 + i * 512, 512) for i in range(2)]
        roped = [view(15360 + i * 256, 256) for i in range(2)]
        probs = sb("probs", [P, 4, PW], F32)
        masked = view(15872, 2 * PW).rearrange("p (i n) -> p i n", i=2)
        probsT = sb("probsT", [P, 2, PW], F32)
        neg_max = sb("neg_max", [P, 2, TPS], F32)
        total = sb("total", [P, 4, TPS], F32)
        inv_total = sb("inv_total", [P, 4, TPS], F32)
        rot_q = view(17408, 2 * SEQ)
        rot_k = view(17920, 2 * SEQ)
        causal = sb("causal", [P, PW], F32)
        hid = [view(i * 512, 512) for i in range(4)]
        hid_hi = [view(2048 + i * 1024, 1024, F16).rearrange("p (f t) -> p f t", f=FB) for i in range(2)]
        hid_lo = [view(4096 + i * 1024, 1024, F16).rearrange("p (f t) -> p f t", f=FB) for i in range(2)]

        bank = [ctx.enter_context(nc.psum_tensor(f"bank{i}", [P, 512], F32)) for i in range(8)]
        PJ, SC, TP, PV = bank[0:2], bank[2:4], bank[4:6], bank[6:8]
        HB, YB = bank[0:4], bank[4:6]

        x_in = [sem(f"x_in{i}") for i in range(NL)]
        wqk_in, wvo_in, w1_in, w2_in, const_in = (sem(n) for n in ("wqk_in", "wvo_in", "w1_in", "w2_in", "const_in"))
        raw_hi, split = sem("raw_hi"), sem("split")
        zeroed, made = sem("zeroed"), sem("made")
        dv = sem("dv")
        centred, squared, var_done, rstd_done, xn_done = (sem(n) for n in ("centred", "squared", "var_done", "rstd_done", "xn_done"))
        xT_ready, xT_hi, xT_done, logits_ready, exp_logits = (sem(n) for n in ("xT_ready", "xT_hi", "xT_done", "logits_ready", "exp_logits"))
        logits_done = sem("logits_done")
        acc_ready = sem("acc_ready")
        pj_ready = sem("pj_ready")
        rest_hi, rest_lo = sem("rest_hi"), sem("rest_lo")
        turn_done, rope_sum, rope_hi, rope_lo = (sem(n) for n in ("turn_done", "rope_sum", "rope_hi", "rope_lo"))
        v_ready = sem("v_ready")
        stacked = [sem(f"stacked{r}") for r in range(GRP)]
        s_ready, s_masked, exp_done, inv_done, p_ready, t_ready, pv_done = (sem(n) for n in (
            "s_ready", "s_masked", "exp_done", "inv_done", "p_ready", "t_ready", "pv_done"))
        t_out = [sem("t_out_dve"), sem("t_out_act")]
        o_hi, o_done = sem("o_hi"), sem("o_done")
        y_done = sem("y_done")
        h_ready, h_gelu, h_hi, y2_ready, y2_done, stored = (sem(n) for n in (
            "h_ready", "h_gelu", "h_hi", "y2_ready", "y2_done", "stored"))
        h_lo = [sem("h_lo_pool"), sem("h_lo_dve")]

        block = ctx.enter_context(nc.Block())

        x_tiles = x.rearrange("b (t p) d -> p (b t) d", p=P)
        out_tiles = out.rearrange("b (t p) d -> p (b t) d", p=P)

        def over_samples(eng, body):
            body(0, True, False)
            with eng.Fori(1, B - 1) as b:
                body(b, False, False)
            body(B - 1, False, True)

        def beside(b, first, last, s):
            return [(kind, j, unit_base(b, first) + n, n)
                    for n, (at, kind, j) in enumerate(units_of(first, last)) if at == s]

        def parts(which, rest, g, n=1):
            at = slice(g * SEQ, (g + n) * SEQ)
            if which == 0:
                return q_staged[:, rest, 0, at], q_staged[:, rest, 1, at]
            return k_staged[:, 0, rest, at], k_staged[:, 1, rest, at]

        def owner(kind, b):
            return b + 1 if kind in NEXT else b - 1 if kind == "y" else b

        def read_out(kind, j, of):
            return {"rest": (rest_lo, 4 * of + j + 1), "rope": (turn_done, 8 * of + j + 1), "v_low": (v_ready, 4 * of + j + 1),
                    "v_high": (v_ready, 4 * of + j + 3), "y": (y_done, 2 * of + j + 1)}[kind]

        def before(b, first, last, n):
            if n < 2:
                return read_out("v_low", n, b)
            _, kind, j = units_of(first, last)[n - 2]
            return read_out(kind, j, owner(kind, b))

        @block.sync
        def _(sp):
            for i in range(NL):
                sp.dma_start(acc[:, i * LC:(i + 1) * LC, :], x_tiles[:, i * LC:(i + 1) * LC, :]).then_inc(x_in[i], 16)
                if i == 0:
                    sp.dma_start(stage_a[:, 0:24 * P], wqk).then_inc(wqk_in, 16)
            sp.dma_start(stage_b[:, 0:H * DK], wv).then_inc(wvo_in, 16)
            sp.dma_start(stage_b[:, H * DK:H * DK + 8 * D], wo).then_inc(wvo_in, 16)
            sp.wait_ge(split, 1)
            sp.dma_start(stage_a, w1).then_inc(w1_in, 16)
            sp.wait_ge(split, 3)
            sp.dma_start(stage_b, w2).then_inc(w2_in, 16)

            def stack(n, r):
                src = slice(32 * r, 32 * r + 32)
                for half_at in range(2):
                    rows = slice(64 * half_at, 64 * half_at + 64)
                    sp.dma_start(k_stack[rows, NG * r:NG * r + NG, :].rearrange("p h t -> p (h t)"),
                                 k_staged[src, half_at, :, :]).then_inc(stacked[r], 16)
                    sp.dma_start(q_stack[rows, r, :, :].rearrange("p l n -> p (l n)"),
                                 q_staged[src, :, :, :].rearrange("p k l n -> p (k l n)")).then_inc(stacked[r], 16)

            sp.wait_ge(rest_lo, 4)
            sp.wait_ge(rope_lo, 8)
            for r in range(GRP):
                stack(0, r)

            def sample(b, first, last):
                if last:
                    return
                sp.wait_ge(rest_lo, 4 * b + 8)
                sp.wait_ge(rope_lo, 8 * b + 16)
                for r in range(GRP):
                    sp.wait_ge(s_ready, 16 * b + 4 * r + 4)
                    stack(b + 1, r)

            over_samples(sp, sample)

            with sp.Fori(0, NC) as c:
                sp.wait_ge(y2_done, E * c + E)
                sp.dma_start(out_tiles[:, bass.ds(c * CT, CT), :], acc[:, bass.ds(c * CT, CT), :]).then_inc(stored, 16)
            sp.wait_ge(stored, 16 * NC)

        @block.gpsimd
        def _(pool):
            pool.dma_start(rw_f[:], rw).then_inc(const_in, 16)
            pool.dma_start(rb_all[:], rb.rearrange("(a e) -> a e", a=1).broadcast_to([P, E + 1])).then_inc(const_in, 16)
            pool.dma_start(rot_q, tables[0]).then_inc(const_in, 16)
            pool.dma_start(rot_k, tables[1]).then_inc(const_in, 16)
            nc.gpsimd.memset(ident[:], 0.0).then_inc(zeroed, 1)
            nc.gpsimd.memset(causal[:], 0.0).then_inc(zeroed, 1)
            nc.gpsimd.memset(half[:], -0.5).then_inc(zeroed, 1)
            for e in range(E + 1):
                nc.gpsimd.memset(rank[:, e:e + 1], float(E + 1 - e)).then_inc(zeroed, 1)
            pool.wait_ge(zeroed, 3)
            nc.gpsimd.affine_select(out=ident[:], in_=ident[:], compare_op=ALU.not_equal, fill=1.0, base=0,
                                    pattern=[[-1, P]], channel_multiplier=1).then_inc(made, 1)
            for at in (0, 2 * P):
                nc.gpsimd.affine_select(out=causal[:, at:at + P], in_=causal[:, at:at + P], compare_op=ALU.is_ge,
                                        fill=MASKED, base=0, pattern=[[-1, P]], channel_multiplier=1).then_inc(made, 1)
            for i in range(NL):
                ts = slice(i * LC, (i + 1) * LC)
                pool.wait_ge(var_done, i + 1)
                nc.gpsimd.tensor_tensor(rstd[:, ts], small[:, 0, ts], half[:, ts], ALU.pow).then_inc(rstd_done, 1)

            def rope_add(n, k):
                if not (isinstance(k, int) and k < 2):
                    pool.wait_ge(rope_lo, k - 1)
                pool.wait_ge(turn_done, k + 1)
                t = turned[n % 2]
                nc.gpsimd.tensor_tensor(roped[n % 2], t[:, 0:SEQ], t[:, SEQ:2 * SEQ], ALU.add).then_inc(rope_sum, 1)

            def rope_low(n, j, k):
                pool.wait_ge(rope_hi, k + 1)
                hi, lo = parts(j // NG, 0, j % NG)
                nc.gpsimd.tensor_tensor(lo, roped[n % 2], hi, ALU.subtract).then_inc(rope_lo, 1)

            for j in range(8):
                rope_add(j, j)
                rope_low(j, j, j)

            def scale(G, s):
                pool.wait_ge(inv_done, G + 1)
                p0, p1 = probs[:, s % 4, 0:P], probs[:, s % 4, P:PW]
                nc.gpsimd.tensor_tensor(p0, p0, inv_total[:, s % 4, 0:1].broadcast_to([P, P]), ALU.mult)
                nc.gpsimd.tensor_scalar(p1, p1, inv_total[:, s % 4, 1:2], 1.0, ALU.mult, ALU.mult).then_inc(p_ready, 1)

            def sample(b, first, last):
                for s in range(H):
                    if not (first and s < INV_LAG):
                        scale(16 * b + s - INV_LAG, s - INV_LAG)
                    for kind, j, u, n in beside(b, first, last, s - 1):
                        if kind == "rope":
                            rope_low(j, j, 8 * b + 8 + j)
                    for kind, j, u, n in beside(b, first, last, s):
                        if kind == "rope":
                            rope_add(j, 8 * b + 8 + j)

            over_samples(pool, sample)
            for lag in range(INV_LAG, 0, -1):
                scale(16 * B - lag, H - lag)

            def chunk(c):
                for e in range(E):
                    for fb in range(0, FB, 2):
                        pool.wait_ge(h_hi, FB * (E * c + e) + fb + 1)
                        nc.gpsimd.tensor_tensor(hid_lo[e % 2][:, fb, :], hid[fb], hid_hi[e % 2][:, fb, :],
                                                ALU.subtract).then_inc(h_lo[0], 1)

            with pool.Fori(0, NC) as c:
                chunk(c)

        @block.scalar
        def _(act):
            def raw(dst, src):
                nc.scalar.activation(dst, src, ACT.Copy, scale=W_SCALE).then_inc(raw_hi, 1)

            act.wait_ge(const_in, 64)
            raw(rw_hi[:], rw_f[:])
            act.wait_ge(wqk_in, 16)
            raw(wqk_hi[:].rearrange("p g n -> p (g n)"), stage_a[:, 0:24 * P])

            def square(i):
                act.wait_ge(centred, i + 1)
                if i >= 1:
                    act.wait_ge(var_done, i)
                nc.scalar.activation(sq, xc[i % 2], ACT.Square).then_inc(squared, 1)

            def xT_high(i):
                for q in range(LQ):
                    n = i * LQ + q
                    act.wait_ge(xT_ready, n + 1)
                    nc.scalar.activation(xnT_hi[:, n * 512:(n + 1) * 512], bank[n % 2][:], ACT.Copy).then_inc(xT_hi, 1)

            for i in range(NL):
                square(i)
                if i >= 1:
                    xT_high(i - 1)
            xT_high(NL - 1)
            act.wait_ge(wvo_in, 32)
            raw(wv_hi[:], stage_b[:, 0:H * DK])
            raw(wo_hi[:].rearrange("p g n -> p (g n)"), stage_b[:, H * DK:H * DK + 8 * D])
            act.wait_ge(w1_in, 16)
            raw(w1_hi[:].rearrange("p g n -> p (g n)"), stage_a)
            act.wait_ge(w2_in, 16)
            raw(w2_hi[:].rearrange("p g f n -> p (g f n)"), stage_b)
            act.wait_ge(logits_done, 1)
            nc.scalar.activation(route[1], route[0], ACT.Exp).then_inc(exp_logits, 1)

            def rest_high(j, u, n, k, samples):
                if j == 0:
                    for r in range(GRP):
                        if samples is not None:
                            act.wait_ge(stacked[r], 64 * samples)
                act.wait_ge(pj_ready, u + 1)
                nc.scalar.activation(parts(j // 2, 1, 2 * (j % 2), 2)[0], PJ[n % 2][:], ACT.Copy,
                                     scale=-UNSCALE / 8 if j < 2 else UNSCALE).then_inc(rest_hi, 1)

            def rope_high(n, j, k):
                act.wait_ge(rope_sum, k + 1)
                nc.scalar.activation(parts(j // NG, 0, j % NG)[0], roped[n % 2], ACT.Copy).then_inc(rope_hi, 1)

            def v_copy(kind, t, u, n, done):
                if done is not None:
                    act.wait_ge(pv_done, done)
                act.wait_ge(pj_ready, u + 1)
                at = 0 if kind == "v_low" else 512
                nc.scalar.activation(v_sb[:, t, at:at + 512], PJ[n % 2][:], ACT.Copy,
                                     scale=UNSCALE).then_inc(v_ready, 1)

            act.wait_ge(acc_ready, 1)
            for n, (kind, j) in enumerate(PROLOGUE):
                if kind == "rest":
                    rest_high(j, n, n, j, None)
                elif kind == "rope":
                    rope_high(j, j, j)
                else:
                    v_copy(kind, j, n, n, None)

            def t_evict(G, s):
                act.wait_ge(t_ready, G + 1)
                if not (isinstance(G, int) and G < 2):
                    act.wait_ge(pv_done, G - 1)
                nc.scalar.activation(probsT[:, s % 2, :], TP[s % 2][:, 0:PW], ACT.Copy).then_inc(t_out[1], 1)

            def o_high(G, s, y_unit):
                act.wait_ge(pv_done, G + 1)
                if y_unit is not None:
                    act.wait_ge(pj_ready, y_unit + 1)
                j = s // 2
                nc.scalar.activation(ot_hi[:, j, :], PV[j % 2][:, 0:SEQ], ACT.Copy).then_inc(o_hi, 1)

            def exps(b, s, first):
                G = 16 * b + s
                act.wait_ge(s_masked, G + 1)
                if not (first and s < 4):
                    act.wait_ge(t_ready, G - 3)
                for t, (at, w) in enumerate(((0, P), (P, 2 * P))):
                    last = nc.scalar.activation(probs[:, s % 4, at:at + w], masked[:, s % 2, at:at + w], ACT.Exp,
                                                bias=neg_max[:, s % 2, t:t + 1], scale=-1.0,
                                                accum_out=total[:, s % 4, t:t + 1])
                last.then_inc(exp_done, 1)

            def late(b, first, last, s):
                G = 16 * b + s
                if not (first and s < T_LAG) and (s - T_LAG) % 2 == 1:
                    t_evict(G - T_LAG, (s - T_LAG) % 2)
                if not (first and s < PV_LAG) and (s - PV_LAG) % 2 == 1:
                    y_unit = None
                    if s == PV_LAG + 1 and not first:
                        y_unit = unit_base(b, first) + [u[1:] for u in units_of(first, last)].index(("y", 1))
                    o_high(G - PV_LAG, (s - PV_LAG) % H, y_unit)

            def sample(b, first, last):
                for s in range(H):
                    exps(b, s, first)
                    for kind, j, u, n in beside(b, first, last, s):
                        if kind == "rest":
                            rest_high(j, u, n, 4 * b + 4 + j, b + 1)
                        elif kind in ("v_low", "v_high"):
                            v_copy(kind, j, u, n, (16 * b + 8 if kind == "v_low" else None if first else 16 * b))
                    for kind, j, u, n in beside(b, first, last, s - 1):
                        if kind == "rope":
                            rope_high(j, j, 8 * b + 8 + j)
                    late(b, first, last, s)

            over_samples(act, sample)
            t_evict(16 * B - 3, 1)
            o_high(16 * B - 3, H - 3, None)
            t_evict(16 * B - 1, 1)
            o_high(16 * B - 1, H - 1, None)

            def chunk(c, first):
                for e in range(E):
                    for fb in range(FB):
                        g = E * c + e
                        act.wait_ge(h_ready, FB * g + fb + 1)
                        if not (first and e == 0):
                            act.wait_ge(h_lo[fb % 2], 2 * g + fb // 2 - 1)
                        nc.scalar.activation(hid[fb], HB[fb][:], ACT.Gelu, scale=UNSCALE).then_inc(h_gelu, 1)

            chunk(0, True)
            with act.Fori(1, NC) as c:
                chunk(c, False)

        @block.vector
        def _(dve):
            steps = [0]

            def step(ins):
                steps[0] += 1
                ins.then_inc(dv, 1)
                dve.wait_ge(dv, steps[0])

            def low(dst, src, hi, n):
                dve.wait_ge(raw_hi, n)
                return nc.vector.scalar_tensor_tensor(dst, src, W_SCALE, hi, ALU.mult, ALU.subtract)

            def per_tile(v):
                return v.unsqueeze(2).broadcast_to([P, LC, D])

            def xT_low(i):
                for q in range(LQ):
                    n = i * LQ + q
                    dve.wait_ge(xT_hi, n + 1)
                    nc.vector.tensor_tensor(xnT_lo[:, n * 512:(n + 1) * 512], bank[n % 2][:],
                                            xnT_hi[:, n * 512:(n + 1) * 512], ALU.subtract).then_inc(xT_done, 1)

            step(low(rw_lo[:], rw_f[:], rw_hi[:], 1))
            for i in range(NL):
                ts = slice(i * LC, (i + 1) * LC)
                dve.wait_ge(x_in[i], 16)
                step(nc.vector.reduce_sum(small[:, 1, ts], acc[:, ts, :], axis=AX.X))
                step(nc.vector.tensor_scalar(mean[:, ts], small[:, 1, ts], 1.0 / D, None, ALU.mult))
                if i >= 2:
                    dve.wait_ge(xT_ready, LQ * (i - 1))
                nc.vector.tensor_tensor(xc[i % 2], acc[:, ts, :], per_tile(mean[:, ts]), ALU.subtract).then_inc(centred, 1)
                if i == 0:
                    low(wqk_lo[:].rearrange("p g n -> p (g n)"), stage_a[:, 0:24 * P],
                        wqk_hi[:].rearrange("p g n -> p (g n)"), 2).then_inc(split, 1)
                if i >= 1:
                    xT_low(i - 1)
                dve.wait_ge(squared, i + 1)
                step(nc.vector.reduce_sum(small[:, 2, ts], sq, axis=AX.X))
                nc.vector.tensor_scalar(small[:, 0, ts], small[:, 2, ts], 1.0 / D, EPS, ALU.mult, ALU.add).then_inc(var_done, 1)
                dve.wait_ge(rstd_done, i + 1)
                dve.wait_ge(centred, i + 1)
                nc.vector.tensor_tensor(xc[i % 2], xc[i % 2], per_tile(rstd[:, ts]), ALU.mult).then_inc(xn_done, 1)
            xT_low(NL - 1)
            dve.wait_ge(wvo_in, 32)
            low(wv_lo[:], stage_b[:, 0:H * DK], wv_hi[:], 3).then_inc(split, 1)
            low(wo_lo[:].rearrange("p g n -> p (g n)"), stage_b[:, H * DK:H * DK + 8 * D],
                wo_hi[:].rearrange("p g n -> p (g n)"), 4).then_inc(split, 1)

            logit, prob, work, pick, both = route
            dve.wait_ge(logits_ready, 1)
            bias = rb_all[:].unsqueeze(1).broadcast_to([P, NT // 2, E + 1])
            for i in range(2):
                last = nc.vector.scalar_tensor_tensor(
                    logit[:, i * NT // 2:(i + 1) * NT // 2, :],
                    bank[4 + i][:, 0:NT // 2 * (E + 1)].rearrange("p (t e) -> p t e", e=E + 1),
                    UNSCALE, bias, ALU.mult, ALU.add)
            step(last)

            def per_expert(v):
                return v.unsqueeze(2).broadcast_to([P, NT, E + 1])

            ranks = rank[:].unsqueeze(1).broadcast_to([P, NT, E + 1])
            best, key = small[:, 0, :], small[:, 1, :]
            step(nc.vector.reduce_max(best, logit, axis=AX.X))
            nc.vector.tensor_tensor(logit, logit, per_expert(best), ALU.subtract).then_inc(logits_done, 1)
            dve.wait_ge(exp_logits, 1)
            step(nc.vector.reduce_sum(best, prob, axis=AX.X))
            step(nc.vector.reciprocal(key, best))
            step(nc.vector.tensor_tensor(prob, prob, per_expert(key), ALU.mult))
            dve.wait_ge(zeroed, 3 + E + 1)
            for n in range(2):
                src = prob if n == 0 else work
                step(nc.vector.reduce_max(best, src, axis=AX.X))
                step(nc.vector.tensor_tensor(pick, src, per_expert(best), ALU.is_ge))
                step(nc.vector.tensor_tensor(pick, pick, ranks, ALU.mult))
                step(nc.vector.reduce_max(key, pick, axis=AX.X))
                step(nc.vector.tensor_tensor(pick, pick, per_expert(key), ALU.is_equal))
                if n == 0:
                    step(nc.vector.scalar_tensor_tensor(work, pick, -4.0, prob, ALU.mult, ALU.add))
                    step(nc.vector.tensor_copy(both, pick))
            step(nc.vector.tensor_tensor(both, both, pick, ALU.add))
            step(nc.vector.tensor_tensor(both, both, prob, ALU.mult))
            step(nc.vector.tensor_scalar(gates[:], both, UNSCALE, None, ALU.mult))
            step(nc.vector.tensor_tensor(small[:, 0, :], both[:, :, E], rstd[:], ALU.mult))
            step(nc.vector.tensor_tensor(small[:, 1, :], small[:, 0, :], mean[:], ALU.mult))
            step(nc.vector.tensor_scalar(small[:, 2, :], small[:, 0, :], 1.0, None, ALU.add))
            for t in range(NT):
                last = nc.vector.tensor_scalar(acc[:, t, :], acc[:, t, :], small[:, 2, t:t + 1], small[:, 1, t:t + 1],
                                               ALU.mult, ALU.subtract)
            dve.wait_ge(w1_in, 16)
            low(w1_lo[:].rearrange("p g n -> p (g n)"), stage_a, w1_hi[:].rearrange("p g n -> p (g n)"), 5)
            dve.wait_ge(w2_in, 16)
            step(low(w2_lo[:].rearrange("p g f n -> p (g f n)"), stage_b, w2_hi[:].rearrange("p g f n -> p (g f n)"), 6))
            nc.vector.tensor_copy(small[:, 3, 0:1], small[:, 2, 0:1]).then_inc(acc_ready, 1)

            def turn(j, u, n, k):
                dve.wait_ge(pj_ready, u + 1)
                if k is not None:
                    dve.wait_ge(rope_sum, k - 1)
                nc.vector.tensor_tensor(turned[j % 2], PJ[n % 2][:], rot_q if j < NG else rot_k,
                                        ALU.mult).then_inc(turn_done, 1)

            def rest_low(j, n, k):
                dve.wait_ge(rest_hi, k + 1)
                hi, lo = parts(j // 2, 1, 2 * (j % 2), 2)
                nc.vector.scalar_tensor_tensor(lo, PJ[n % 2][:], -UNSCALE / 8 if j < 2 else UNSCALE, hi,
                                               ALU.mult, ALU.subtract).then_inc(rest_lo, 1)

            for n, (kind, j) in enumerate(PROLOGUE):
                if kind == "rest":
                    rest_low(j, n, j)
                elif kind == "rope":
                    turn(j, n, n, None if j < 2 else j)

            def mask(b, s, first):
                G = 16 * b + s
                dve.wait_ge(s_ready, G + 1)
                if not (first and s < INV_LAG):
                    invert(G - INV_LAG, s - INV_LAG)
                for t, (at, w) in enumerate(((0, P), (P, 2 * P))):
                    last = nc.vector.tensor_tensor_reduce(
                        out=masked[:, s % 2, at:at + w], in0=SC[s % 2][:, at:at + w], in1=causal[:, at:at + w],
                        scale=1.0, scalar=MASKED, op0=ALU.add, op1=ALU.min, accum_out=neg_max[:, s % 2, t:t + 1])
                last.then_inc(s_masked, 1)

            def invert(G, s):
                dve.wait_ge(exp_done, G + 1)
                nc.vector.reciprocal(inv_total[:, s % 4, :], total[:, s % 4, :]).then_inc(inv_done, 1)

            def t_evict(G, s):
                dve.wait_ge(t_ready, G + 1)
                if G is not None and not (isinstance(G, int) and G < 2):
                    dve.wait_ge(pv_done, G - 1)
                nc.vector.tensor_copy(probsT[:, s % 2, :], TP[s % 2][:, 0:PW]).then_inc(t_out[0], 1)

            def o_low(J, s):
                dve.wait_ge(o_hi, J + 1)
                j = s // 2
                nc.vector.tensor_tensor(ot_lo[:, j, :], PV[j % 2][:, 0:SEQ], ot_hi[:, j, :],
                                        ALU.subtract).then_inc(o_done, 1)

            def y_add(b, t, u, n):
                dve.wait_ge(pj_ready, u + 1)
                tile = b * TPS + t
                a = acc[:, tile, :] if isinstance(tile, int) else acc[:, bass.ds(tile, 1), :].rearrange("p a d -> p (a d)")
                nc.vector.scalar_tensor_tensor(a, PJ[n % 2][:, 0:D], UNSCALE, a, ALU.mult,
                                               ALU.add).then_inc(y_done, 1)

            def sample(b, first, last):
                for s in range(H):
                    G = 16 * b + s
                    mask(b, s, first)
                    for kind, j, u, n in beside(b, first, last, s):
                        if kind == "rope":
                            turn(j, u, n, 8 * b + 8 + j)
                        elif kind == "rest":
                            rest_low(j, n, 4 * b + 4 + j)
                        elif kind == "y":
                            y_add(b - 1, j, u, n)
                    if not (first and s < T_LAG) and (s - T_LAG) % 2 == 0:
                        t_evict(G - T_LAG, (s - T_LAG) % 2)
                    if not (first and s < PV_LAG) and (s - PV_LAG) % 2 == 1:
                        o_low(8 * b + (s - PV_LAG - 1) // 2, (s - PV_LAG) % H)

            over_samples(dve, sample)
            for lag in range(INV_LAG, 0, -1):
                invert(16 * B - lag, H - lag)
            o_low(8 * B - 2, H - 3)
            t_evict(16 * B - 2, 0)
            o_low(8 * B - 1, H - 1)
            for t in range(TPS):
                y_add(B - 1, t, unit_base(B - 1, False) + len(units_of(False, True)) + t, t)

            def chunk(c, first):
                def gather(g, e, cc):
                    if not (isinstance(g, int) and g == 0):
                        dve.wait_ge(y2_done, g)
                    dve.wait_ge(y2_ready, g + 1)
                    for t in range(CT):
                        tile = cc * CT + t
                        if isinstance(tile, int):
                            a, gate = acc[:, tile, :], gates[:, tile, e:e + 1]
                        else:
                            a = acc[:, bass.ds(tile, 1), :].rearrange("p a d -> p (a d)")
                            gate = gates[:, bass.ds(tile, 1), e:e + 1].rearrange("p a d -> p (a d)")
                        last = nc.vector.scalar_tensor_tensor(a, YB[e % 2][:, t * D:(t + 1) * D], gate, a, ALU.mult, ALU.add)
                    last.then_inc(y2_done, 1)

                for e in range(E):
                    for fb in range(FB):
                        g = E * c + e
                        if fb == 0 and not (first and e < 2):
                            dve.wait_ge(y2_ready, g - 1)
                        dve.wait_ge(h_gelu, FB * g + fb + 1)
                        nc.vector.tensor_copy(hid_hi[e % 2][:, fb, :], hid[fb]).then_inc(h_hi, 1)
                        if fb % 2 == 1:
                            dve.wait_ge(h_hi, FB * g + fb + 1)
                            nc.vector.tensor_tensor(hid_lo[e % 2][:, fb, :], hid[fb], hid_hi[e % 2][:, fb, :],
                                                    ALU.subtract).then_inc(h_lo[1], 1)
                    if not (first and e == 0):
                        gather(E * c + e - 1, (e - 1) % E, c if e > 0 else c - 1)
                return gather

            dve.wait_ge(y_done, TPS * B)
            chunk(0, True)
            with dve.Fori(1, NC) as c:
                gather = chunk(c, False)
            gather(E * NC - 1, E - 1, NC - 1)

        @block.tensor
        def _(pe):
            mm = nc.tensor.matmul

            def split3(dst, a_hi, a_lo, b_hi, b_lo, start=True, stop=True):
                mm(dst, a_hi, b_lo, start=start, stop=False)
                mm(dst, a_lo, b_hi, start=False, stop=False)
                return mm(dst, a_hi, b_hi, start=False, stop=stop)

            pe.wait_ge(made, 3)
            for i in range(NL):
                pe.wait_ge(xn_done, i + 1)
                for q in range(LQ):
                    n = i * LQ + q
                    if n >= 2:
                        pe.wait_ge(xT_done, n - 1)
                    for t in range(4):
                        last = nc.tensor.transpose(bank[n % 2][:, t * P:(t + 1) * P], xc[i % 2][:, q * 4 + t, :], ident[:])
                    last.then_inc(xT_ready, 1)
            pe.wait_ge(xT_done, NL * LQ)
            for t in range(NT):
                at = t % (NT // 2) * (E + 1)
                ts = slice(t * P, (t + 1) * P)
                last = split3(bank[4 + t // (NT // 2)][:, at:at + E + 1], xnT_hi[:, ts], xnT_lo[:, ts], rw_hi[:], rw_lo[:])
            last.then_inc(logits_ready, 1)

            def unit(kind, j, b, n, free):
                if free is not None:
                    pe.wait_ge(*free)
                dst = PJ[n % 2]
                if kind == "y":
                    pe.wait_ge(o_done, 8 * b + 8)
                    for g in range(8):
                        last = split3(dst[:, 0:D], ot_hi[:, g, j * P:(j + 1) * P], ot_lo[:, g, j * P:(j + 1) * P],
                                      wo_hi[:, g, :], wo_lo[:, g, :], start=(g == 0), stop=(g == 7))
                elif kind in ("v_low", "v_high"):
                    ts = bass.ds(b * SEQ + j * P, P)
                    at = 0 if kind == "v_low" else 512
                    last = split3(dst[:], xnT_hi[:, ts], xnT_lo[:, ts], wv_hi[:, at:at + 512], wv_lo[:, at:at + 512])
                else:
                    ts = bass.ds(b * SEQ, SEQ)
                    if kind == "rope":
                        pair = (4 * (j // NG) * 2 + j % NG, 16 + j)
                    else:
                        first_g = 4 + 8 * (j // 2) + 2 * (j % 2)
                        pair = (first_g, first_g + 1)
                    for i, g in enumerate(pair):
                        last = split3(dst[:, i * SEQ:(i + 1) * SEQ], wqk_hi[:, g, :], wqk_lo[:, g, :],
                                      xnT_hi[:, ts], xnT_lo[:, ts])
                last.then_inc(pj_ready, 1)

            pe.wait_ge(acc_ready, 1)
            for n, (kind, j) in enumerate(PROLOGUE):
                unit(kind, j, 0, n, None if n < 2 else read_out(*PROLOGUE[n - 2], 0))

            def scores(b, s, first):
                G = 16 * b + s
                if s % GRP == 0:
                    pe.wait_ge(stacked[s // GRP], 64 * b + 64)
                if not (first and s < 2):
                    pe.wait_ge(s_masked, G - 1)
                for at, w in ((0, P), (P, 2 * P)):
                    qs = slice(0, P) if at == 0 else slice(P, 2 * P)
                    dst = SC[s % 2][:, at:at + w]
                    q_lo, q_hi = (q_stack[:, s // NG, l, s % NG * SEQ + qs.start:s % NG * SEQ + qs.stop] for l in (1, 0))
                    mm(dst, q_lo, k_stack[:, s, 0:w], start=True, stop=False)
                    last = mm(dst, q_hi, k_stack[:, s, 0:w], start=False, stop=True)
                last.then_inc(s_ready, 1)

            def transposes(G, s, evicted):
                pe.wait_ge(p_ready, G + 1)
                if evicted is not None:
                    pe.wait_ge(t_out[s % 2], evicted)
                for k in range(3):
                    last = nc.tensor.transpose(TP[s % 2][:, k * P:(k + 1) * P], probs[:, s % 4, k * P:(k + 1) * P], ident[:])
                last.then_inc(t_ready, 1)

            def attend(b, s, first):
                G, j = 16 * b + s, s // 2
                if s % 8 == 0:
                    pe.wait_ge(v_ready, 4 * b + (2 if s == 0 else 4))
                pe.wait_ge(t_out[s % 2], 8 * b + j + 1)
                if s % 2 == 0 and not (first and j < 2):
                    pe.wait_ge(o_done, 8 * b + j - 1)
                rows = slice(64 * (s % 2), 64 * (s % 2) + 64)
                vs = slice(s * DK, (s + 1) * DK)
                mm(PV[j % 2][rows, 0:SEQ], v_sb[:, 0, vs], probsT[:, s % 2, 0:SEQ], start=True, stop=False)
                mm(PV[j % 2][rows, P:SEQ], v_sb[:, 1, vs], probsT[:, s % 2, SEQ:PW], start=False, stop=True).then_inc(pv_done, 1)

            def sample(b, first, last):
                for s in range(H):
                    G = 16 * b + s
                    scores(b, s, first)
                    for kind, j, u, n in beside(b, first, last, s):
                        unit(kind, j, owner(kind, b), n, before(b, first, last, n))
                    if not (first and s < T_LAG):
                        transposes(G - T_LAG, (s - T_LAG) % 4, None if first and s < T_LAG + 2 else 8 * b + (s - T_LAG) // 2)
                    if s >= PV_LAG:
                        attend(b, s - PV_LAG, first)
                    elif not first:
                        attend(b - 1, s - PV_LAG + H, False)

            over_samples(pe, sample)
            tail = 16 * B
            for lag in range(PV_LAG, 0, -1):
                if lag < PV_LAG:
                    transposes(tail - lag, -lag % 4, 8 * B - (lag + 1) // 2)
                attend(B - 1, H - lag, False)
            n = len(units_of(False, True))
            for t in range(TPS):
                unit("y", t, B - 1, n + t, before(B - 1, False, True, n + t))

            def hidden(c, e, first):
                g = E * c + e
                ts = bass.ds(c * CH, CH)
                for fb in range(FB):
                    if not (first and e == 0):
                        pe.wait_ge(h_gelu, FB * g + fb - FB + 1)
                    fs = slice(fb * P, (fb + 1) * P)
                    split3(HB[fb][:], w1_hi[:, e, fs], w1_lo[:, e, fs], xnT_hi[:, ts], xnT_lo[:, ts]).then_inc(h_ready, 1)

            def down(g, e, first):
                for made_by in h_lo:
                    pe.wait_ge(made_by, 2 * g + 2)
                if not (first and e < 2):
                    pe.wait_ge(y2_done, g - 1)
                for t in range(CT):
                    ts = slice(t * P, (t + 1) * P)
                    for fb in range(FB):
                        last = split3(YB[e % 2][:, t * D:(t + 1) * D], hid_hi[e % 2][:, fb, ts], hid_lo[e % 2][:, fb, ts],
                                      w2_hi[:, e, fb, :], w2_lo[:, e, fb, :], start=(fb == 0), stop=(fb == FB - 1))
                last.then_inc(y2_ready, 1)

            def chunk(c, first):
                for e in range(E):
                    hidden(c, e, first)
                    if e > 0:
                        down(E * c + e - 1, e - 1, first)
                    elif not first:
                        down(E * c - 1, E - 1, False)

            pe.wait_ge(y_done, TPS * B)
            chunk(0, True)
            with pe.Fori(1, NC) as c:
                chunk(c, False)
            down(E * NC - 1, E - 1, False)


def rotation_tables(np):
    inv = (1.0 / np.power(np.float32(6000.0), np.arange(0, ROPE, 2, dtype=np.float32) / np.float32(ROPE))).astype(np.float32)
    angle = np.outer(np.arange(SEQ, dtype=np.float32), inv).astype(np.float32)
    angle = np.concatenate([angle, angle], axis=1).T.astype(np.float64)
    sign = np.where(np.arange(ROPE) < ROPE // 2, -1.0, 1.0)[:, None]
    one = np.concatenate([np.cos(angle).astype(np.float32), (sign * np.sin(angle)).astype(np.float32)], axis=1)
    one = np.tile(one, (GRP, 1))
    return np.stack([one * np.float32(-UNSCALE / 8), one * np.float32(UNSCALE)]).astype(np.float32)


def kernel(**inputs):
    import numpy as np
    import concourse.bacc as bacc
    from concourse.bass_utils import run_bass_kernel_spmd

    wqkv, wo = np.asarray(inputs["L0_attn_W_qkv"]), np.asarray(inputs["L0_attn_W_o"])
    order = [GRP * g + r for r in range(GRP) for g in range(NG)]
    swap = list(range(ROPE // 2, ROPE)) + list(range(ROPE // 2))
    groups = []
    for which in (0, 1):
        for part in (slice(0, ROPE), slice(ROPE, DK)):
            groups += [wqkv[which, GRP * g:GRP * g + GRP, part].reshape(P, D) for g in range(NG)]
    for which in (0, 1):
        groups += [wqkv[which, GRP * g:GRP * g + GRP][:, swap].reshape(P, D) for g in range(NG)]
    arrays = {
        "x": np.ascontiguousarray(inputs["L0_attn_x"]),
        "wqk": np.ascontiguousarray(np.concatenate(groups).T),
        "wv": np.ascontiguousarray(wqkv[2][order].reshape(H * DK, D).T),
        "wo": np.ascontiguousarray(wo.reshape(D, H, DK)[:, order].reshape(D, 8, P).transpose(2, 1, 0).reshape(P, 8 * D)),
        "rw": np.ascontiguousarray(inputs["L0_ffn_router_w"]),
        "rb": np.ascontiguousarray(inputs["L0_ffn_router_b"]),
        "w1": np.ascontiguousarray(np.asarray(inputs["L0_ffn_w1"]).transpose(1, 0, 2).reshape(D, E * F)),
        "w2": np.ascontiguousarray(np.asarray(inputs["L0_ffn_w2"]).reshape(E, FB, P, D).transpose(2, 0, 1, 3).reshape(P, E * FB * D)),
        "tables": rotation_tables(np),
    }
    nc = bacc.Bacc("TRN2", target_bir_lowering=False, num_devices=1)
    args = [nc.dram_tensor(f"{n}_dram", a.shape, F32, kind="ExternalInput").ap() for n, a in arrays.items()]
    out = nc.dram_tensor("out_dram", (B, SEQ, D), F32, kind="ExternalOutput").ap()
    attention_and_experts(nc, *args, out)
    r = run_bass_kernel_spmd(nc, [{f"{n}_dram": a for n, a in arrays.items()}], core_ids=[0])
    return r.results[0]["out_dram"]
```

```python
from contextlib import ExitStack

import concourse.bass as bass
from concourse import mybir

F32 = mybir.dt.float32
F16 = mybir.dt.float16
ALU = mybir.AluOpType
ACT = mybir.ActivationFunctionType
AX = mybir.AxisListType

P = 128
B, SEQ, D = 32, 256, 128
H, DK = 16, 64
ROPE = DK // 2
E, F = 8, 512
NT = B * SEQ // P
TPS = SEQ // P
GRP = 4
NG = H // GRP
FB = F // P
CH = 512
NC = B * SEQ // CH
CT = CH // P
LC = 16
NL = NT // LC
LQ = LC // 4
W_SCALE = 64.0
UNSCALE = 1.0 / W_SCALE
EPS = 1e-5
MASKED = 3.0e38
PW = P + 2 * P

PROLOGUE = ([("rest", 0), ("rest", 1)] + [("rope", j) for j in range(4)]
            + [("rest", 2), ("rest", 3)] + [("rope", j) for j in range(4, 8)] + [("v_low", 0), ("v_low", 1)])
BESIDE = [
    [("rest", 0)], [("rest", 1), ("rope", 0)], [("rope", 1)], [("rope", 2), ("rope", 3)],
    [("rest", 2)], [("rest", 3), ("rope", 4)], [], [("rope", 5), ("rope", 6)],
    [("rope", 7)], [("v_high", 0), ("v_high", 1)], [], [("y", 0)],
    [("v_low", 0)], [("y", 1)], [("v_low", 1)], [],
]
NEXT = ("rest", "rope", "v_low")
PJ_BANKS = 3
INV_LAG, T_LAG, OUT_LAG, PV_LAG, O_LAG = 2, 3, 4, 5, 6


def units_of(first, last):
    out = []
    for s, units in enumerate(BESIDE):
        for kind, j in units:
            if (first and kind == "y") or (last and kind in NEXT):
                continue
            out.append((s, kind, j))
    return out


FULL = len(units_of(False, False))
OPEN = len(PROLOGUE) + len(units_of(True, False))


assert FULL % PJ_BANKS == 0 and OPEN % PJ_BANKS == 0


def unit_base(b, first):
    return len(PROLOGUE) if first else OPEN + FULL * (b - 1)


def attention_and_experts(nc, x, wqk, wvo, rw, rb, experts, tables, out):
    with ExitStack() as ctx:
        def sb(name, shape, dt):
            return ctx.enter_context(nc.sbuf_tensor(name, shape, dt))

        def sem(name):
            return ctx.enter_context(nc.semaphore(name))

        acc = sb("acc", [P, NT, D], F32)
        xnT_hi = sb("xnT_hi", [P, NT * P], F16)
        xnT_lo = sb("xnT_lo", [P, NT * P], F16)
        wqk_hi = sb("wqk_hi", [P, 24, P], F16)
        wqk_lo = sb("wqk_lo", [P, 24, P], F16)
        wvo_hi = sb("wvo_hi", [P, 2, H * DK], F16)
        wvo_lo = sb("wvo_lo", [P, 2, H * DK], F16)
        wv_hi, wv_lo = wvo_hi[:, 0, :], wvo_lo[:, 0, :]
        wo_hi, wo_lo = (w[:, 1, :].rearrange("p (j d) -> p j d", j=8) for w in (wvo_hi, wvo_lo))
        rw_f = sb("rw_f", [P, E + 1], F32)
        rw_hi = sb("rw_hi", [P, E + 1], F16)
        rw_lo = sb("rw_lo", [P, E + 1], F16)
        rb_all = sb("rb_all", [P, E + 1], F32)
        gates = sb("gates", [P, NT, E + 1], F32)
        ident = sb("ident", [P, P], F32)
        rank = sb("rank", [P, E + 1], F32)
        neg_mean = sb("neg_mean", [P, NT], F32)
        rstd = sb("rstd", [P, NT], F32)
        small = sb("small", [P, 4, NT], F32)
        half = sb("half", [P, NT], F32)
        arena = sb("arena", [P, 18 * 1024], F32)
        second = sb("second", [P, 8 * 1024], F32)

        def view(at, words, dt=F32, of=arena):
            v = of[:, at:at + words]
            return v if dt == F32 else v.bitcast(dt)

        raw_qk = view(0, 24 * P)
        raw_vo = view(4096, 2 * H * DK)
        xn = [view(8192 + i * 2048, 2048).rearrange("p (t d) -> p t d", d=D) for i in range(2)]
        route = [view(6144 + i * 576, 576).rearrange("p (t e) -> p t e", e=E + 1) for i in range(3)]
        k_stack = [view(0, 2048, F16, of).rearrange("p (h t) -> p h t", t=SEQ) for of in (arena, second)]
        q_stack = [view(2048, 4096, F16, of).rearrange("p (r l n) -> p r l n", r=GRP, l=2) for of in (arena, second)]
        v_sb = view(6144, 2048, F32, second).rearrange("p (t n) -> p t n", t=TPS)
        q_staged = view(8192, 2048, F16).rearrange("p (k l n) -> p k l n", k=2, l=2)
        k_staged = view(10240, 2048, F16).rearrange("p (l k n) -> p l k n", k=2, l=2)
        ot_hi = [view(at, 1024, F16).rearrange("p (j t) -> p j t", j=8) for at in (12288, 6144)]
        ot_lo = [view(at, 1024, F16).rearrange("p (j t) -> p j t", j=8) for at in (13312, 7168)]
        turned = [view(14336 + i * 512, 512) for i in range(2)]
        roped = [view(at, 256) for at in (15360, 15616, 16640, 16896)]
        probs = sb("probs", [P, 4, PW], F32)
        masked = view(15872, 2 * PW).rearrange("p (i n) -> p i n", i=2)
        probsT = sb("probsT", [P, 4, PW], F32)
        neg_max = sb("neg_max", [P, 2, TPS], F32)
        total = sb("total", [P, 4, TPS], F32)
        inv_total = sb("inv_total", [P, 4, TPS], F32)
        rot_q = view(17408, 2 * SEQ)
        rot_k = view(17920, 2 * SEQ)
        causal = sb("causal", [P, PW], F32)
        raw_e = [view(8192 + e * 2 * F if e < 6 else 6144 + (e - 6) * 2 * F, 2 * F) for e in range(E)]
        w_hi = view(0, E * F, F16, second).rearrange("p (e k f) -> p e k f", e=E, k=2)
        w_lo = view(E * F, E * F, F16, second).rearrange("p (e k f) -> p e k f", e=E, k=2)
        hid = [view(i * 512, 512) for i in range(4)]
        hid_hi = [view(2048 + i * 1024, 1024, F16).rearrange("p (f t) -> p f t", f=FB) for i in range(2)]
        hid_lo = [view(4096 + i * 1024, 1024, F16).rearrange("p (f t) -> p f t", f=FB) for i in range(2)]

        bank = [ctx.enter_context(nc.psum_tensor(f"bank{i}", [P, 512], F32)) for i in range(8)]
        PJ, SC, TP = bank[0:3], bank[3:5], bank[5:7]
        PV = bank[7][:, 0:SEQ]
        LG = bank[6:8]
        HB, YB = bank[0:4], bank[4:6]

        x_in = [sem(f"x_in{i}") for i in range(NL)]
        wqk_in, wvo_in, const_in = sem("wqk_in"), sem("wvo_in"), sem("const_in")
        raw_in = [sem(f"raw_in{e}") for e in range(E)]
        raw_hi, split = sem("raw_hi"), sem("split")
        zeroed, made = sem("zeroed"), sem("made")
        dv = sem("dv")
        mean_done, squared, var_done, rstd_done, xn_done = (sem(n) for n in ("mean_done", "squared", "var_done", "rstd_done", "xn_done"))
        xT_ready, xT_hi, xT_done, logits_ready, exp_logits = (sem(n) for n in ("xT_ready", "xT_hi", "xT_done", "logits_ready", "exp_logits"))
        logits_done, mixed = sem("logits_done"), sem("mixed")
        pj_ready = sem("pj_ready")
        rest_hi, rest_lo = sem("rest_hi"), sem("rest_lo")
        turn_done, rope_sum, rope_hi = (sem(n) for n in ("turn_done", "rope_sum", "rope_hi"))
        q_rope_lo, k_rope_lo = sem("q_rope_lo"), sem("k_rope_lo")
        v_ready = sem("v_ready")
        q_stacked = [sem(f"q_stacked{r}") for r in range(GRP)]
        k_stacked = [sem(f"k_stacked{r}") for r in range(GRP)]
        s_ready, s_masked, exp_done, inv_done, p_ready, t_ready, pv_done = (sem(n) for n in (
            "s_ready", "s_masked", "exp_done", "inv_done", "p_ready", "t_ready", "pv_done"))
        t_out = [sem("t_out_dve"), sem("t_out_act")]
        o_hi, o_done = sem("o_hi"), sem("o_done")
        y_done = sem("y_done")
        h_ready, h_gelu, h_hi, y2_ready, y2_done, stored = (sem(n) for n in (
            "h_ready", "h_gelu", "h_hi", "y2_ready", "y2_done", "stored"))
        h_lo = [sem("h_lo_pool"), sem("h_lo_dve")]

        block = ctx.enter_context(nc.Block())

        x_tiles = x.rearrange("b (t p) d -> p (b t) d", p=P)
        out_tiles = out.rearrange("b (t p) d -> p (b t) d", p=P)

        def over_samples(eng, body):
            body(0, 0, True, False)
            with eng.Fori(0, B // 2 - 1) as i:
                body(2 * i + 1, 1, False, False)
                body(2 * i + 2, 0, False, False)
            body(B - 1, 1, False, True)

        def beside(b, first, last, s):
            return [(kind, j, unit_base(b, first) + n, PJ[(n + (len(PROLOGUE) if first else 0)) % PJ_BANKS], n)
                    for n, (at, kind, j) in enumerate(units_of(first, last)) if at == s]

        def parts(which, rest, g, n=1):
            at = slice(g * SEQ, (g + n) * SEQ)
            if which == 0:
                return q_staged[:, rest, 0, at], q_staged[:, rest, 1, at]
            return k_staged[:, 0, rest, at], k_staged[:, 1, rest, at]

        def owner(kind, b):
            return b + 1 if kind in NEXT else b - 1 if kind == "y" else b

        def read_out(kind, j, of):
            return {"rest": (rest_lo, 4 * of + j + 1), "rope": (turn_done, 8 * of + j + 1), "v_low": (v_ready, 4 * of + j + 1),
                    "v_high": (v_ready, 4 * of + j + 3), "y": (y_done, 2 * of + j + 1)}[kind]

        def before(b, first, last, n):
            if n >= PJ_BANKS:
                _, kind, j = units_of(first, last)[n - PJ_BANKS]
                return read_out(kind, j, owner(kind, b))
            if first:
                return read_out(*PROLOGUE[n - PJ_BANKS], 0)
            _, kind, j = units_of(False, False)[n - PJ_BANKS]
            return read_out(kind, j, owner(kind, b - 1))

        @block.sync
        def _(sp):
            for i in range(NL):
                sp.dma_start(acc[:, i * LC:(i + 1) * LC, :], x_tiles[:, i * LC:(i + 1) * LC, :]).then_inc(x_in[i], 16)
                if i == 1:
                    sp.dma_start(raw_qk, wqk).then_inc(wqk_in, 16)
            sp.dma_start(raw_vo, wvo).then_inc(wvo_in, 16)

            def load_expert(e):
                sp.dma_start(raw_e[e], experts[:, e * 2 * F:(e + 1) * 2 * F]).then_inc(raw_in[e], 16)

            def stack_q(n, parity):
                sp.wait_ge(q_rope_lo, 4 * n + 4)
                for r in range(GRP):
                    for half_at in range(2):
                        sp.dma_start(q_stack[parity][64 * half_at:64 * half_at + 64, r, :, :].rearrange("p l n -> p (l n)"),
                                     q_staged[32 * r:32 * r + 32, :, :, :].rearrange("p k l n -> p (k l n)")).then_inc(q_stacked[r], 16)

            def stack_k(n, parity):
                sp.wait_ge(k_rope_lo, 4 * n + 4)
                for r in range(GRP):
                    for half_at in range(2):
                        sp.dma_start(k_stack[parity][64 * half_at:64 * half_at + 64, NG * r:NG * r + NG, :].rearrange("p h t -> p (h t)"),
                                     k_staged[32 * r:32 * r + 32, half_at, :, :]).then_inc(k_stacked[r], 16)

            sp.wait_ge(split, 2)
            stack_q(0, 0)
            stack_k(0, 0)

            def sample(b, parity, first, last):
                if not last:
                    stack_q(b + 1, 1 - parity)
                    stack_k(b + 1, 1 - parity)
                    return
                for r in range(GRP):
                    sp.wait_ge(q_stacked[r], 32 * B)
                    sp.wait_ge(k_stacked[r], 32 * B)
                for e in range(4):
                    load_expert(e)
                sp.wait_ge(y_done, TPS * (B - 1))
                for e in range(4, 6):
                    load_expert(e)

            over_samples(sp, sample)
            sp.wait_ge(y_done, TPS * B)
            for e in range(6, E):
                load_expert(e)

            with sp.Fori(0, NC) as c:
                sp.wait_ge(y2_done, E * c + E)
                sp.dma_start(out_tiles[:, bass.ds(c * CT, CT), :], acc[:, bass.ds(c * CT, CT), :]).then_inc(stored, 16)
            sp.wait_ge(stored, 16 * NC)

        @block.gpsimd
        def _(pool):
            pool.dma_start(rw_f[:], rw).then_inc(const_in, 16)
            pool.dma_start(rb_all[:], rb.rearrange("(a e) -> a e", a=1).broadcast_to([P, E + 1])).then_inc(const_in, 16)
            pool.dma_start(rot_q, tables[0]).then_inc(const_in, 16)
            pool.dma_start(rot_k, tables[1]).then_inc(const_in, 16)
            nc.gpsimd.memset(ident[:], 0.0).then_inc(zeroed, 1)
            nc.gpsimd.memset(causal[:], 0.0).then_inc(zeroed, 1)
            nc.gpsimd.memset(half[:], -0.5).then_inc(zeroed, 1)
            for e in range(E + 1):
                nc.gpsimd.memset(rank[:, e:e + 1], float(E + 1 - e)).then_inc(zeroed, 1)
            pool.wait_ge(zeroed, 3)
            nc.gpsimd.affine_select(out=ident[:], in_=ident[:], compare_op=ALU.not_equal, fill=1.0, base=0,
                                    pattern=[[-1, P]], channel_multiplier=1).then_inc(made, 1)
            for at in (0, 2 * P):
                nc.gpsimd.affine_select(out=causal[:, at:at + P], in_=causal[:, at:at + P], compare_op=ALU.is_ge,
                                        fill=MASKED, base=0, pattern=[[-1, P]], channel_multiplier=1).then_inc(made, 1)
            for i in range(NL):
                ts = slice(i * LC, (i + 1) * LC)
                pool.wait_ge(var_done, i + 1)
                nc.gpsimd.tensor_tensor(rstd[:, ts], small[:, 0, ts], half[:, ts], ALU.pow).then_inc(rstd_done, 1)

            def rope_add(j, m):
                if j >= 4:
                    pool.wait_ge(q_rope_lo, 4 * m + j - 3)
                elif not (isinstance(m, int) and m == 0):
                    pool.wait_ge(k_rope_lo, 4 * m + j - 3)
                pool.wait_ge(turn_done, 8 * m + j + 1)
                t = turned[j % 2]
                nc.gpsimd.tensor_tensor(roped[j % 4], t[:, 0:SEQ], t[:, SEQ:2 * SEQ], ALU.add).then_inc(rope_sum, 1)

            def q_rope_low(j, m):
                pool.wait_ge(rope_hi, 8 * m + j + 1)
                hi, lo = parts(0, 0, j)
                nc.gpsimd.tensor_tensor(lo, roped[j], hi, ALU.subtract).then_inc(q_rope_lo, 1)

            for j in range(8):
                rope_add(j, 0)
                if 1 <= j <= NG:
                    q_rope_low(j - 1, 0)

            def scale(G, s):
                pool.wait_ge(inv_done, G + 1)
                p0, p1 = probs[:, s % 4, 0:P], probs[:, s % 4, P:PW]
                nc.gpsimd.tensor_tensor(p0, p0, inv_total[:, s % 4, 0:1].broadcast_to([P, P]), ALU.mult)
                nc.gpsimd.tensor_scalar(p1, p1, inv_total[:, s % 4, 1:2], 1.0, ALU.mult, ALU.mult).then_inc(p_ready, 1)

            def sample(b, parity, first, last):
                for s in range(H):
                    if not (first and s < INV_LAG):
                        scale(16 * b + s - INV_LAG, s - INV_LAG)
                    for kind, j, u, psum, n in beside(b, first, last, s - 3):
                        if kind == "rope" and j < NG:
                            q_rope_low(j, b + 1)
                    for kind, j, u, psum, n in beside(b, first, last, s - 1):
                        if kind == "rope":
                            rope_add(j, b + 1)

            over_samples(pool, sample)
            for lag in range(INV_LAG, 0, -1):
                scale(16 * B - lag, H - lag)

            def chunk(c):
                for e in range(E):
                    for fb in range(0, FB, 2):
                        pool.wait_ge(h_hi, FB * (E * c + e) + fb + 1)
                        nc.gpsimd.tensor_tensor(hid_lo[e % 2][:, fb, :], hid[fb], hid_hi[e % 2][:, fb, :],
                                                ALU.subtract).then_inc(h_lo[0], 1)

            with pool.Fori(0, NC) as c:
                chunk(c)

        @block.scalar
        def _(act):
            def raw(dst, src):
                nc.scalar.activation(dst, src, ACT.Copy, scale=W_SCALE).then_inc(raw_hi, 1)

            act.wait_ge(const_in, 64)
            raw(rw_hi[:], rw_f[:])

            def square(i):
                act.wait_ge(mean_done, i + 1)
                for t in range(LC):
                    at = i * LC + t
                    last = nc.scalar.activation(xn[i % 2][:, t, :], acc[:, at, :], ACT.Square, bias=neg_mean[:, at:at + 1],
                                                accum_out=small[:, 2, at:at + 1])
                last.then_inc(squared, 1)

            def xT_high(i):
                for q in range(LQ):
                    n = i * LQ + q
                    act.wait_ge(xT_ready, n + 1)
                    nc.scalar.activation(xnT_hi[:, n * 512:(n + 1) * 512], bank[n % 4][:], ACT.Copy).then_inc(xT_hi, 1)

            for i in range(NL):
                square(i)
                if i >= 1:
                    xT_high(i - 1)
                if i == 1:
                    act.wait_ge(wqk_in, 16)
                    raw(wqk_hi[:].rearrange("p g n -> p (g n)"), raw_qk)
                if i == 2:
                    act.wait_ge(wvo_in, 16)
                    raw(wvo_hi[:].rearrange("p k n -> p (k n)"), raw_vo)
            xT_high(NL - 1)

            def rest_high(j, u, psum, m, staged_before):
                if staged_before:
                    if j % 2 == 0:
                        for done in (q_stacked if j < 2 else k_stacked):
                            act.wait_ge(done, 32 * m)
                act.wait_ge(pj_ready, u + 1)
                nc.scalar.activation(parts(j // 2, 1, 2 * (j % 2), 2)[0], psum[:], ACT.Copy,
                                     scale=-UNSCALE / 8 if j < 2 else UNSCALE).then_inc(rest_hi, 1)

            def rope_high(j, m):
                act.wait_ge(rope_sum, 8 * m + j + 1)
                nc.scalar.activation(parts(j // NG, 0, j % NG)[0], roped[j % 4], ACT.Copy).then_inc(rope_hi, 1)

            def v_copy(kind, t, u, psum, done):
                if done is not None:
                    act.wait_ge(pv_done, done)
                act.wait_ge(pj_ready, u + 1)
                at = 0 if kind == "v_low" else 512
                nc.scalar.activation(v_sb[:, t, at:at + 512], psum[:], ACT.Copy, scale=UNSCALE).then_inc(v_ready, 1)

            for n, (kind, j) in enumerate(PROLOGUE):
                if kind == "rest":
                    rest_high(j, n, PJ[n % PJ_BANKS], 0, False)
                elif kind == "rope":
                    rope_high(j, 0)
                else:
                    v_copy(kind, j, n, PJ[n % PJ_BANKS], None)

            def t_evict(G, s):
                act.wait_ge(t_ready, G + 1)
                if not (isinstance(G, int) and G < 4):
                    act.wait_ge(pv_done, G - 3)
                nc.scalar.activation(probsT[:, s % 4, :], TP[s % 2][:, 0:PW], ACT.Copy).then_inc(t_out[1], 1)

            def o_high(G, s, parity):
                act.wait_ge(pv_done, G + 1)
                nc.scalar.activation(ot_hi[parity][:, s // 2, :], PV, ACT.Copy).then_inc(o_hi, 1)

            def exps(b, s, first):
                G = 16 * b + s
                act.wait_ge(s_masked, G + 1)
                if not (first and s < 4):
                    act.wait_ge(t_ready, G - 3)
                for t, (at, w) in enumerate(((0, P), (P, 2 * P))):
                    last = nc.scalar.activation(probs[:, s % 4, at:at + w], masked[:, s % 2, at:at + w], ACT.Exp,
                                                bias=neg_max[:, s % 2, t:t + 1], scale=-1.0,
                                                accum_out=total[:, s % 4, t:t + 1])
                last.then_inc(exp_done, 1)

            def sample(b, parity, first, last):
                for s in range(H):
                    for kind, j, u, psum, n in beside(b, first, last, s - 1):
                        if kind == "rest":
                            rest_high(j, u, psum, b + 1, True)
                        elif kind in ("v_low", "v_high"):
                            v_copy(kind, j, u, psum, (16 * b + 8 if kind == "v_low" else None if first else 16 * b))
                    if not (first and s < O_LAG) and (s - O_LAG) % 2 == 1:
                        o_high(16 * b + s - O_LAG, (s - O_LAG) % H, parity if s >= O_LAG else 1 - parity)
                    if not (first and s < OUT_LAG) and (s - OUT_LAG) % 2 == 1:
                        t_evict(16 * b + s - OUT_LAG, (s - OUT_LAG) % 4)
                    exps(b, s, first)
                    for kind, j, u, psum, n in beside(b, first, last, s - 2):
                        if kind == "rope":
                            rope_high(j, b + 1)
                    if first and s == 3:
                        act.wait_ge(logits_done, 1)
                        nc.scalar.activation(route[1], route[0], ACT.Exp).then_inc(exp_logits, 1)

            over_samples(act, sample)
            last = (B - 1) % 2
            t_evict(16 * B - 3, 1)
            o_high(16 * B - 5, H - 5, last)
            t_evict(16 * B - 1, 3)
            o_high(16 * B - 3, H - 3, last)
            o_high(16 * B - 1, H - 1, last)

            def split_high(e):
                act.wait_ge(raw_in[e], 16)
                nc.scalar.activation(w_hi[:, e, :, :].rearrange("p k f -> p (k f)"), raw_e[e],
                                     ACT.Copy, scale=W_SCALE).then_inc(raw_hi, 1)

            act.wait_ge(y_done, TPS * B)
            split_high(0)
            split_high(1)

            def chunk(c, first):
                for e in range(E):
                    for fb in range(FB):
                        g = E * c + e
                        act.wait_ge(h_ready, FB * g + fb + 1)
                        if not (first and e == 0):
                            act.wait_ge(h_lo[fb % 2], 2 * g + fb // 2 - 1)
                        nc.scalar.activation(hid[fb], HB[fb][:], ACT.Gelu, scale=UNSCALE).then_inc(h_gelu, 1)
                    if first and e + 2 < E:
                        split_high(e + 2)

            chunk(0, True)
            with act.Fori(1, NC) as c:
                chunk(c, False)

        @block.vector
        def _(dve):
            steps = [0]

            def step(ins):
                steps[0] += 1
                ins.then_inc(dv, 1)
                dve.wait_ge(dv, steps[0])

            def low(dst, src, hi, n):
                dve.wait_ge(raw_hi, n)
                return nc.vector.scalar_tensor_tensor(dst, src, W_SCALE, hi, ALU.mult, ALU.subtract)

            def xT_low(i):
                for q in range(LQ):
                    n = i * LQ + q
                    dve.wait_ge(xT_hi, n + 1)
                    nc.vector.tensor_tensor(xnT_lo[:, n * 512:(n + 1) * 512], bank[n % 4][:],
                                            xnT_hi[:, n * 512:(n + 1) * 512], ALU.subtract).then_inc(xT_done, 1)

            def means(i):
                ts = slice(i * LC, (i + 1) * LC)
                dve.wait_ge(x_in[i], 16)
                step(nc.vector.reduce_sum(small[:, 1, ts], acc[:, ts, :], axis=AX.X))
                nc.vector.tensor_scalar(neg_mean[:, ts], small[:, 1, ts], -1.0 / D, None, ALU.mult).then_inc(mean_done, 1)

            def normalise(i):
                ts = slice(i * LC, (i + 1) * LC)
                dve.wait_ge(squared, i + 1)
                nc.vector.tensor_scalar(small[:, 0, ts], small[:, 2, ts], 1.0 / D, EPS, ALU.mult, ALU.add).then_inc(var_done, 1)
                if i >= 1:
                    xT_low(i - 1)
                dve.wait_ge(rstd_done, i + 1)
                for t in range(LC):
                    at = i * LC + t
                    last = nc.vector.tensor_scalar(xn[i % 2][:, t, :], acc[:, at, :], neg_mean[:, at:at + 1], rstd[:, at:at + 1],
                                                   ALU.add, ALU.mult)
                last.then_inc(xn_done, 1)

            means(0)
            for i in range(NL):
                if i + 1 < NL:
                    means(i + 1)
                if i == 0:
                    low(rw_lo[:], rw_f[:], rw_hi[:], 1).then_inc(dv, 1)
                    steps[0] += 1
                normalise(i)
                if i == 1:
                    low(wqk_lo[:].rearrange("p g n -> p (g n)"), raw_qk,
                        wqk_hi[:].rearrange("p g n -> p (g n)"), 2).then_inc(split, 1)
            low(wvo_lo[:].rearrange("p k n -> p (k n)"), raw_vo, wvo_hi[:].rearrange("p k n -> p (k n)"), 3).then_inc(split, 1)
            xT_low(NL - 1)

            logit, prob, pick = route
            both = logit
            best, key = small[:, 0, :], small[:, 1, :]

            def per_expert(v):
                return v.unsqueeze(2).broadcast_to([P, NT, E + 1])

            def router_logits():
                dve.wait_ge(logits_ready, 1)
                bias = rb_all[:].unsqueeze(1).broadcast_to([P, NT // 2, E + 1])
                for i in range(2):
                    last = nc.vector.scalar_tensor_tensor(
                        logit[:, i * NT // 2:(i + 1) * NT // 2, :],
                        LG[i][:, 0:NT // 2 * (E + 1)].rearrange("p (t e) -> p t e", e=E + 1),
                        UNSCALE, bias, ALU.mult, ALU.add)
                step(last)
                step(nc.vector.reduce_max(best, logit, axis=AX.X))
                nc.vector.tensor_tensor(logit, logit, per_expert(best), ALU.subtract).then_inc(logits_done, 1)

            def router_softmax():
                dve.wait_ge(exp_logits, 1)
                step(nc.vector.reduce_sum(best, prob, axis=AX.X))
                step(nc.vector.reciprocal(key, best))
                step(nc.vector.tensor_tensor(prob, prob, per_expert(key), ALU.mult))

            def router_choice(n):
                ranks = rank[:].unsqueeze(1).broadcast_to([P, NT, E + 1])
                if n == 0:
                    dve.wait_ge(zeroed, 3 + E + 1)
                step(nc.vector.reduce_max(best, prob, axis=AX.X))
                step(nc.vector.tensor_tensor(pick, prob, per_expert(best), ALU.is_ge))
                step(nc.vector.tensor_tensor(pick, pick, ranks, ALU.mult))
                step(nc.vector.reduce_max(key, pick, axis=AX.X))
                step(nc.vector.tensor_tensor(pick, pick, per_expert(key), ALU.is_equal))
                if n == 0:
                    step(nc.vector.tensor_tensor(both, pick, prob, ALU.mult))
                    step(nc.vector.scalar_tensor_tensor(prob, pick, -4.0, prob, ALU.mult, ALU.add))
                else:
                    step(nc.vector.tensor_tensor(pick, pick, prob, ALU.mult))
                    step(nc.vector.tensor_tensor(both, both, pick, ALU.add))

            def router_gates():
                step(nc.vector.tensor_scalar(gates[:], both, UNSCALE, None, ALU.mult))
                step(nc.vector.tensor_tensor(small[:, 0, :], both[:, :, E], rstd[:], ALU.mult))
                step(nc.vector.tensor_tensor(small[:, 1, :], small[:, 0, :], neg_mean[:], ALU.mult))
                step(nc.vector.tensor_scalar(small[:, 2, :], small[:, 0, :], 1.0, None, ALU.add))

            def mix(b):
                for t in range(TPS):
                    tile = b * TPS + t
                    if isinstance(tile, int):
                        a, c1, c0 = acc[:, tile, :], small[:, 2, tile:tile + 1], small[:, 1, tile:tile + 1]
                    else:
                        a, c1, c0 = (v[:, bass.ds(tile, 1), :].rearrange("p a d -> p (a d)")
                                     for v in (acc, small[:, 2, :].unsqueeze(2), small[:, 1, :].unsqueeze(2)))
                    last = nc.vector.tensor_scalar(a, a, c1, c0, ALU.mult, ALU.add)
                last.then_inc(mixed, 1)

            def turn(j, u, psum, m):
                dve.wait_ge(pj_ready, u + 1)
                if not (isinstance(m, int) and m == 0 and j < 2):
                    dve.wait_ge(rope_sum, 8 * m + j - 1)
                nc.vector.tensor_tensor(turned[j % 2], psum[:], rot_q if j < NG else rot_k,
                                        ALU.mult).then_inc(turn_done, 1)

            def rest_low(j, psum, m):
                dve.wait_ge(rest_hi, 4 * m + j + 1)
                hi, lo = parts(j // 2, 1, 2 * (j % 2), 2)
                nc.vector.scalar_tensor_tensor(lo, psum[:], -UNSCALE / 8 if j < 2 else UNSCALE, hi,
                                               ALU.mult, ALU.subtract).then_inc(rest_lo, 1)

            def k_rope_low(j, m):
                dve.wait_ge(rope_hi, 8 * m + j + 1)
                hi, lo = parts(1, 0, j - NG)
                nc.vector.tensor_tensor(lo, roped[j % 4], hi, ALU.subtract).then_inc(k_rope_lo, 1)

            for n, (kind, j) in enumerate(PROLOGUE):
                if kind == "rest":
                    rest_low(j, PJ[n % PJ_BANKS], 0)
                elif kind == "rope":
                    turn(j, n, PJ[n % PJ_BANKS], 0)
                    if j >= NG + 2:
                        k_rope_low(j - 2, 0)
            k_rope_low(6, 0)
            k_rope_low(7, 0)

            def mask(b, s, first):
                G = 16 * b + s
                dve.wait_ge(s_ready, G + 1)
                if not (first and s < INV_LAG):
                    invert(G - INV_LAG, s - INV_LAG)
                for t, (at, w) in enumerate(((0, P), (P, 2 * P))):
                    last = nc.vector.tensor_tensor_reduce(
                        out=masked[:, s % 2, at:at + w], in0=SC[s % 2][:, at:at + w], in1=causal[:, at:at + w],
                        scale=1.0, scalar=MASKED, op0=ALU.add, op1=ALU.min, accum_out=neg_max[:, s % 2, t:t + 1])
                last.then_inc(s_masked, 1)

            def invert(G, s):
                dve.wait_ge(exp_done, G + 1)
                nc.vector.reciprocal(inv_total[:, s % 4, :], total[:, s % 4, :]).then_inc(inv_done, 1)

            def t_evict(G, s):
                dve.wait_ge(t_ready, G + 1)
                if not (isinstance(G, int) and G < 4):
                    dve.wait_ge(pv_done, G - 3)
                nc.vector.tensor_copy(probsT[:, s % 4, :], TP[s % 2][:, 0:PW]).then_inc(t_out[0], 1)

            def o_low(J, s, parity):
                dve.wait_ge(o_hi, J + 1)
                j = s // 2
                nc.vector.tensor_tensor(ot_lo[parity][:, j, :], PV, ot_hi[parity][:, j, :], ALU.subtract).then_inc(o_done, 1)

            def y_add(b, t, u, psum):
                dve.wait_ge(mixed, b + 1)
                dve.wait_ge(pj_ready, u + 1)
                tile = b * TPS + t
                a = acc[:, tile, :] if isinstance(tile, int) else acc[:, bass.ds(tile, 1), :].rearrange("p a d -> p (a d)")
                nc.vector.scalar_tensor_tensor(a, psum[:, 0:D], UNSCALE, a, ALU.mult, ALU.add).then_inc(y_done, 1)

            def sample(b, parity, first, last):
                for s in range(H):
                    G = 16 * b + s
                    mask(b, s, first)
                    if not (first and s < O_LAG) and (s - O_LAG) % 2 == 1:
                        o_low(8 * b + (s - O_LAG - 1) // 2, (s - O_LAG) % H, parity if s >= O_LAG else 1 - parity)
                    for kind, j, u, psum, n in beside(b, first, last, s - 3):
                        if kind == "rope" and j >= NG:
                            k_rope_low(j, b + 1)
                    for kind, j, u, psum, n in beside(b, first, last, s - 1):
                        if kind == "rope":
                            turn(j, u, psum, b + 1)
                        elif kind == "rest":
                            rest_low(j, psum, b + 1)
                        elif kind == "y":
                            y_add(b - 1, j, u, psum)
                    if s == 4 and not first:
                        mix(b - 1)
                    if not (first and s < OUT_LAG) and (s - OUT_LAG) % 2 == 0:
                        t_evict(G - OUT_LAG, (s - OUT_LAG) % 4)
                    if first:
                        if s == 2:
                            router_logits()
                        elif s == 5:
                            router_softmax()
                        elif s == 8:
                            router_choice(0)
                        elif s == 11:
                            router_choice(1)
                        elif s == 13:
                            router_gates()

            over_samples(dve, sample)
            parity = (B - 1) % 2
            invert(16 * B - 2, H - 2)
            t_evict(16 * B - 4, 0)
            invert(16 * B - 1, H - 1)
            o_low(8 * B - 3, H - 5, parity)
            t_evict(16 * B - 2, 2)
            o_low(8 * B - 2, H - 3, parity)
            mix(B - 1)
            o_low(8 * B - 1, H - 1, parity)
            for t in range(TPS):
                n = len(units_of(False, True)) + t
                y_add(B - 1, t, unit_base(B - 1, False) + n, PJ[n % PJ_BANKS])

            def split_low(e):
                low(w_lo[:, e, :, :].rearrange("p k f -> p (k f)"), raw_e[e],
                    w_hi[:, e, :, :].rearrange("p k f -> p (k f)"), 4 + e).then_inc(split, 1)

            def chunk(c, first):
                def gather(g, e, cc):
                    if not (isinstance(g, int) and g == 0):
                        dve.wait_ge(y2_done, g)
                    dve.wait_ge(y2_ready, g + 1)
                    for t in range(CT):
                        tile = cc * CT + t
                        if isinstance(tile, int):
                            a, gate = acc[:, tile, :], gates[:, tile, e:e + 1]
                        else:
                            a = acc[:, bass.ds(tile, 1), :].rearrange("p a d -> p (a d)")
                            gate = gates[:, bass.ds(tile, 1), e:e + 1].rearrange("p a d -> p (a d)")
                        last = nc.vector.scalar_tensor_tensor(a, YB[e % 2][:, t * D:(t + 1) * D], gate, a, ALU.mult, ALU.add)
                    last.then_inc(y2_done, 1)

                for e in range(E):
                    for fb in range(FB):
                        g = E * c + e
                        if fb == 0 and not (first and e < 2):
                            dve.wait_ge(y2_ready, g - 1)
                        dve.wait_ge(h_gelu, FB * g + fb + 1)
                        nc.vector.tensor_copy(hid_hi[e % 2][:, fb, :], hid[fb]).then_inc(h_hi, 1)
                        if fb % 2 == 1:
                            dve.wait_ge(h_hi, FB * g + fb + 1)
                            nc.vector.tensor_tensor(hid_lo[e % 2][:, fb, :], hid[fb], hid_hi[e % 2][:, fb, :],
                                                    ALU.subtract).then_inc(h_lo[1], 1)
                    if first and e + 2 < E:
                        split_low(e + 2)
                    if not (first and e == 0):
                        gather(E * c + e - 1, (e - 1) % E, c if e > 0 else c - 1)
                return gather

            dve.wait_ge(y_done, TPS * B)
            split_low(0)
            split_low(1)
            chunk(0, True)
            with dve.Fori(1, NC) as c:
                gather = chunk(c, False)
            gather(E * NC - 1, E - 1, NC - 1)

        @block.tensor
        def _(pe):
            mm = nc.tensor.matmul

            def split3(dst, a_hi, a_lo, b_hi, b_lo, start=True, stop=True):
                mm(dst, a_hi, b_lo, start=start, stop=False)
                mm(dst, a_lo, b_hi, start=False, stop=False)
                return mm(dst, a_hi, b_hi, start=False, stop=stop)

            pe.wait_ge(made, 3)
            def logits(i):
                pe.wait_ge(xT_done, (i + 1) * LQ)
                for t in range(i * LC, (i + 1) * LC):
                    at = t % (NT // 2) * (E + 1)
                    ts = slice(t * P, (t + 1) * P)
                    last = split3(LG[t // (NT // 2)][:, at:at + E + 1], xnT_hi[:, ts], xnT_lo[:, ts], rw_hi[:], rw_lo[:])
                return last

            for i in range(NL):
                pe.wait_ge(xn_done, i + 1)
                for q in range(LQ):
                    n = i * LQ + q
                    if n >= 4:
                        pe.wait_ge(xT_done, n - 3)
                    for t in range(4):
                        last = nc.tensor.transpose(bank[n % 4][:, t * P:(t + 1) * P], xn[i % 2][:, q * 4 + t, :], ident[:])
                    last.then_inc(xT_ready, 1)
                if i >= 1:
                    logits(i - 1)
            logits(NL - 1).then_inc(logits_ready, 1)

            def unit(kind, j, b, parity, dst, free):
                if free is not None:
                    pe.wait_ge(*free)
                if kind == "y":
                    pe.wait_ge(o_done, 8 * b + 8)
                    for g in range(8):
                        last = split3(dst[:, 0:D], ot_hi[parity][:, g, j * P:(j + 1) * P], ot_lo[parity][:, g, j * P:(j + 1) * P],
                                      wo_hi[:, g, :], wo_lo[:, g, :], start=(g == 0), stop=(g == 7))
                elif kind in ("v_low", "v_high"):
                    ts = bass.ds(b * SEQ + j * P, P)
                    at = 0 if kind == "v_low" else 512
                    last = split3(dst[:], xnT_hi[:, ts], xnT_lo[:, ts], wv_hi[:, at:at + 512], wv_lo[:, at:at + 512])
                else:
                    ts = bass.ds(b * SEQ, SEQ)
                    if kind == "rope":
                        pair = (4 * (j // NG) * 2 + j % NG, 16 + j)
                    else:
                        first_g = 4 + 8 * (j // 2) + 2 * (j % 2)
                        pair = (first_g, first_g + 1)
                    for i, g in enumerate(pair):
                        last = split3(dst[:, i * SEQ:(i + 1) * SEQ], wqk_hi[:, g, :], wqk_lo[:, g, :],
                                      xnT_hi[:, ts], xnT_lo[:, ts])
                last.then_inc(pj_ready, 1)

            pe.wait_ge(split, 2)
            for n, (kind, j) in enumerate(PROLOGUE):
                unit(kind, j, 0, 0, PJ[n % PJ_BANKS], None if n < PJ_BANKS else read_out(*PROLOGUE[n - PJ_BANKS], 0))

            def scores(b, s, parity, first):
                G = 16 * b + s
                if s % GRP == 0:
                    pe.wait_ge(q_stacked[s // GRP], 32 * b + 32)
                    pe.wait_ge(k_stacked[s // GRP], 32 * b + 32)
                if not (first and s < 2):
                    pe.wait_ge(s_masked, G - 1)
                for at, w in ((0, P), (P, 2 * P)):
                    qs = slice(0, P) if at == 0 else slice(P, 2 * P)
                    dst = SC[s % 2][:, at:at + w]
                    q_lo, q_hi = (q_stack[parity][:, s // NG, l, s % NG * SEQ + qs.start:s % NG * SEQ + qs.stop] for l in (1, 0))
                    mm(dst, q_lo, k_stack[parity][:, s, 0:w], start=True, stop=False)
                    last = mm(dst, q_hi, k_stack[parity][:, s, 0:w], start=False, stop=True)
                last.then_inc(s_ready, 1)

            def transposes(G, s, evicted):
                pe.wait_ge(p_ready, G + 1)
                if evicted is not None:
                    pe.wait_ge(t_out[s % 2], evicted)
                for k in range(3):
                    last = nc.tensor.transpose(TP[s % 2][:, k * P:(k + 1) * P], probs[:, s % 4, k * P:(k + 1) * P], ident[:])
                last.then_inc(t_ready, 1)

            def attend(b, j, first):
                if j % 4 == 0:
                    pe.wait_ge(v_ready, 4 * b + (2 if j == 0 else 4))
                if not (first and j < 1):
                    pe.wait_ge(o_done, 8 * b + j)
                for i in range(2):
                    s = 2 * j + i
                    pe.wait_ge(t_out[i], 8 * b + j + 1)
                    rows = slice(64 * i, 64 * i + 64)
                    vs = slice(s * DK, (s + 1) * DK)
                    mm(PV[rows, :], v_sb[:, 0, vs], probsT[:, s % 4, 0:SEQ], start=True, stop=False)
                    mm(PV[rows, P:SEQ], v_sb[:, 1, vs], probsT[:, s % 4, SEQ:PW], start=False, stop=True).then_inc(pv_done, 1)

            def sample(b, parity, first, last):
                for s in range(H):
                    G = 16 * b + s
                    scores(b, s, parity, first)
                    for kind, j, u, psum, n in beside(b, first, last, s):
                        unit(kind, j, owner(kind, b), parity if kind == "v_high" else 1 - parity, psum, before(b, first, last, n))
                    if not (first and s < T_LAG):
                        transposes(G - T_LAG, (s - T_LAG) % 4, None if first and s < T_LAG + 2 else 8 * b + (s - T_LAG) // 2)
                    if (s - PV_LAG) % 2 == 1:
                        if s > PV_LAG:
                            attend(b, (s - PV_LAG) // 2, first)
                        elif not first:
                            attend(b - 1, (s - PV_LAG + H) // 2, False)

            over_samples(pe, sample)
            for s in range(H, H + PV_LAG):
                if s < H + T_LAG:
                    transposes(16 * (B - 1) + s - T_LAG, (s - T_LAG) % 4, 8 * (B - 1) + (s - T_LAG) // 2)
                if (s - PV_LAG) % 2 == 1:
                    attend(B - 1, (s - PV_LAG) // 2, False)
            for t in range(TPS):
                n = len(units_of(False, True)) + t
                unit("y", t, B - 1, (B - 1) % 2, PJ[n % PJ_BANKS], before(B - 1, False, True, n))

            def hidden(c, e, first):
                g = E * c + e
                ts = bass.ds(c * CH, CH)
                if first:
                    pe.wait_ge(split, 2 + e + 1)
                for fb in range(FB):
                    if not (first and e == 0):
                        pe.wait_ge(h_gelu, FB * g + fb - FB + 1)
                    fs = slice(fb * P, (fb + 1) * P)
                    split3(HB[fb][:], w_hi[:, e, 0, fs], w_lo[:, e, 0, fs], xnT_hi[:, ts], xnT_lo[:, ts]).then_inc(h_ready, 1)

            def down(g, e, first):
                for made_by in h_lo:
                    pe.wait_ge(made_by, 2 * g + 2)
                if not (first and e < 2):
                    pe.wait_ge(y2_done, g - 1)
                for t in range(CT):
                    ts = slice(t * P, (t + 1) * P)
                    for fb in range(FB):
                        last = split3(YB[e % 2][:, t * D:(t + 1) * D], hid_hi[e % 2][:, fb, ts], hid_lo[e % 2][:, fb, ts],
                                      w_hi[:, e, 1, fb * D:(fb + 1) * D], w_lo[:, e, 1, fb * D:(fb + 1) * D], start=(fb == 0), stop=(fb == FB - 1))
                last.then_inc(y2_ready, 1)

            def chunk(c, first):
                for e in range(E):
                    hidden(c, e, first)
                    if e > 0:
                        down(E * c + e - 1, e - 1, first)
                    elif not first:
                        down(E * c - 1, E - 1, False)

            pe.wait_ge(y_done, TPS * B)
            chunk(0, True)
            with pe.Fori(1, NC) as c:
                chunk(c, False)
            down(E * NC - 1, E - 1, False)


def rotation_tables(np):
    inv = (1.0 / np.power(np.float32(6000.0), np.arange(0, ROPE, 2, dtype=np.float32) / np.float32(ROPE))).astype(np.float32)
    angle = np.outer(np.arange(SEQ, dtype=np.float32), inv).astype(np.float32)
    angle = np.concatenate([angle, angle], axis=1).T.astype(np.float64)
    sign = np.where(np.arange(ROPE) < ROPE // 2, -1.0, 1.0)[:, None]
    one = np.concatenate([np.cos(angle).astype(np.float32), (sign * np.sin(angle)).astype(np.float32)], axis=1)
    one = np.tile(one, (GRP, 1))
    return np.stack([one * np.float32(-UNSCALE / 8), one * np.float32(UNSCALE)]).astype(np.float32)


def kernel(**inputs):
    import numpy as np
    import concourse.bacc as bacc
    from concourse.bass_utils import run_bass_kernel_spmd

    wqkv, wo = np.asarray(inputs["L0_attn_W_qkv"]), np.asarray(inputs["L0_attn_W_o"])
    order = [GRP * g + r for r in range(GRP) for g in range(NG)]
    swap = list(range(ROPE // 2, ROPE)) + list(range(ROPE // 2))
    groups = []
    for which in (0, 1):
        for part in (slice(0, ROPE), slice(ROPE, DK)):
            groups += [wqkv[which, GRP * g:GRP * g + GRP, part].reshape(P, D) for g in range(NG)]
    for which in (0, 1):
        groups += [wqkv[which, GRP * g:GRP * g + GRP][:, swap].reshape(P, D) for g in range(NG)]
    arrays = {
        "x": np.ascontiguousarray(inputs["L0_attn_x"]),
        "wqk": np.ascontiguousarray(np.concatenate(groups).T),
        "wvo": np.ascontiguousarray(np.concatenate([
            wqkv[2][order].reshape(H * DK, D).T,
            wo.reshape(D, H, DK)[:, order].reshape(D, 8, P).transpose(2, 1, 0).reshape(P, 8 * D)], axis=1)),
        "rw": np.ascontiguousarray(inputs["L0_ffn_router_w"]),
        "rb": np.ascontiguousarray(inputs["L0_ffn_router_b"]),
        "experts": np.ascontiguousarray(np.concatenate([
            np.asarray(inputs["L0_ffn_w1"]).transpose(1, 0, 2),
            np.asarray(inputs["L0_ffn_w2"]).reshape(E, FB, P, D).transpose(2, 0, 1, 3).reshape(P, E, FB * D)], axis=2).reshape(P, E * 2 * F)),
        "tables": rotation_tables(np),
    }
    nc = bacc.Bacc("TRN2", target_bir_lowering=False, num_devices=1)
    args = [nc.dram_tensor(f"{n}_dram", a.shape, F32, kind="ExternalInput").ap() for n, a in arrays.items()]
    out = nc.dram_tensor("out_dram", (B, SEQ, D), F32, kind="ExternalOutput").ap()
    attention_and_experts(nc, *args, out)
    r = run_bass_kernel_spmd(nc, [{f"{n}_dram": a for n, a in arrays.items()}], core_ids=[0])
    return r.results[0]["out_dram"]
```

```python
from contextlib import ExitStack

import concourse.bass as bass
from concourse import mybir

F32 = mybir.dt.float32
F16 = mybir.dt.float16
I16 = mybir.dt.int16
I32 = mybir.dt.int32
ALU = mybir.AluOpType
ACT = mybir.ActivationFunctionType
AX = mybir.AxisListType

P = 128
B, SEQ, D = 32, 256, 128
H, DK = 16, 64
ROPE = DK // 2
E, F = 8, 512
NT = B * SEQ // P
TPS = SEQ // P
GRP = 4
NG = H // GRP
FB = F // P
TOP = 2
PARTS = (44, 20)
ET = 2 * P
MAX_T = max(PARTS) * P // ET
PART_T = [TOP * n * P // ET + E for n in PARTS]
TILES = sum(PART_T)
NS = E * len(PARTS)
SPARE = P
ROWS = SPARE + TILES * ET
BODY = 4
BITS = E.bit_length() - 1
COMBINE_AT = PART_T[0] // BODY
COMBINED = (0, 2, 2, 2)
RING = sum(COMBINED)
LC = 16
NL = NT // LC
LQ = LC // 4
W_SCALE = 64.0
UNSCALE = 1.0 / W_SCALE
EPS = 1e-5
MASKED = 3.0e38
PW = P + 2 * P

PROLOGUE = ([("rest", 0), ("rest", 1)] + [("rope", j) for j in range(4)]
            + [("rest", 2), ("rest", 3)] + [("rope", j) for j in range(4, 8)] + [("v_low", 0), ("v_low", 1)])
BESIDE = [
    [("rest", 0)], [("rest", 1), ("rope", 0)], [("rope", 1)], [("rope", 2), ("rope", 3)],
    [("rest", 2)], [("rest", 3), ("rope", 4)], [], [("rope", 5), ("rope", 6)],
    [("rope", 7)], [("v_high", 0), ("v_high", 1)], [], [("y", 0)],
    [("v_low", 0)], [("y", 1)], [("v_low", 1)], [],
]
SEND_AT = [1, 9, 12, 14]
NEXT = ("rest", "rope", "v_low")
PJ_BANKS = 3
INV_LAG, T_LAG, OUT_LAG, PV_LAG, O_LAG = 2, 3, 4, 5, 6


def units_of(first, last):
    out = []
    for s, units in enumerate(BESIDE):
        for kind, j in units:
            if (first and kind == "y") or (last and kind in NEXT):
                continue
            out.append((s, kind, j))
    return out


FULL = len(units_of(False, False))
OPEN = len(PROLOGUE) + len(units_of(True, False))


assert FULL % PJ_BANKS == 0 and OPEN % PJ_BANKS == 0


def unit_base(b, first):
    return len(PROLOGUE) if first else OPEN + FULL * (b - 1)


def attention_and_experts(nc, x, wqk, wvo, rw, rb, experts, tables, sorted_x, sorted_y, out):
    with ExitStack() as ctx:
        def sb(name, shape, dt):
            return ctx.enter_context(nc.sbuf_tensor(name, shape, dt))

        def sem(name):
            return ctx.enter_context(nc.semaphore(name))

        acc = sb("acc", [P, NT, D], F32)
        xnT_hi = sb("xnT_hi", [P, NT * P], F16)
        xnT_lo = sb("xnT_lo", [P, NT * P], F16)
        wqk_hi = sb("wqk_hi", [P, 24, P], F16)
        wqk_lo = sb("wqk_lo", [P, 24, P], F16)
        wvo_hi = sb("wvo_hi", [P, 2, H * DK], F16)
        wvo_lo = sb("wvo_lo", [P, 2, H * DK], F16)
        wv_hi, wv_lo = wvo_hi[:, 0, :], wvo_lo[:, 0, :]
        wo_hi, wo_lo = (w[:, 1, :].rearrange("p (j d) -> p j d", j=8) for w in (wvo_hi, wvo_lo))
        rw_f = sb("rw_f", [P, E + 1], F32)
        rw_hi = sb("rw_hi", [P, E + 1], F16)
        rw_lo = sb("rw_lo", [P, E + 1], F16)
        rb_all = sb("rb_all", [P, E + 1], F32)
        gates = sb("gates", [P, NT, TOP], F32)
        slots = sb("slots", [P, NT, TOP], I32)
        body_experts = sb("body_experts", [1, TILES // BODY], I16)
        send_x = sb("send_x", [P, TPS, D], F32)
        send_at = sb("send_at", [P, TPS * TOP], I32)
        lane_i = sb("lane_i", [P, 1], I32)
        grid_i = sb("grid_i", [P, max(PART_T)], I32)
        ident = sb("ident", [P, P], F32)
        rank = sb("rank", [P, E + 1], F32)
        neg_mean = sb("neg_mean", [P, NT], F32)
        rstd = sb("rstd", [P, NT], F32)
        small = sb("small", [P, 4, NT], F32)
        half = sb("half", [P, NT], F32)
        arena = sb("arena", [P, 18 * 1024], F32)
        second = sb("second", [P, 8 * 1024], F32)

        def view(at, words, dt=F32, of=arena):
            v = of[:, at:at + words]
            return v if dt == F32 else v.bitcast(dt)

        raw_qk = view(0, 24 * P)
        raw_vo = view(4096, 2 * H * DK)
        xn = [view(8192 + i * 2048, 2048).rearrange("p (t d) -> p t d", d=D) for i in range(2)]
        prob, logit, pick0, pick1 = (view(i * 576, 576).rearrange("p (t e) -> p t e", e=E + 1) for i in range(4))
        below, ones = view(3072, P), view(3072 + P, P)
        zero_rows = view(3072 + 2 * P, D)
        scan = [view(4096 + i * 512, 512) for i in range(2)]
        by_slot = view(5120, 512).rearrange("p (t e) -> p t e", e=E)
        fills = view(5632, NS * MAX_T).rearrange("p (s k) -> p s k", k=MAX_T)
        names, at = {}, 5632 + NS * MAX_T
        for name, words in (("held", NS), ("behind_all", 2 * NS), ("tiles", NS), ("base", NS), ("start", NS + len(PARTS)),
                            ("lane", 1), ("grid", max(PART_T)), ("bounds", MAX_T), ("owner", TILES), ("packed", TILES // BODY)):
            names[name] = view(at, words)
            at += words

        def by_part(v):
            return v.rearrange("p (e h) -> p e h", h=len(PARTS))

        held, behind_all, tiles, base, start = (names[n] for n in ("held", "behind_all", "tiles", "base", "start"))
        lane, grid, bounds, owner_f, packed = (names[n] for n in ("lane", "grid", "bounds", "owner", "packed"))
        k_stack = [view(0, 2048, F16, of).rearrange("p (h t) -> p h t", t=SEQ) for of in (second, arena)]
        q_stack = [view(2048, 4096, F16, of).rearrange("p (r l n) -> p r l n", r=GRP, l=2) for of in (second, arena)]
        v_sb = view(6144, 2048, F32, second).rearrange("p (t n) -> p t n", t=TPS)
        q_staged = view(8192, 2048, F16).rearrange("p (k l n) -> p k l n", k=2, l=2)
        k_staged = view(10240, 2048, F16).rearrange("p (l k n) -> p l k n", k=2, l=2)
        ot_hi = [view(at, 1024, F16).rearrange("p (j t) -> p j t", j=8) for at in (12288, 6144)]
        ot_lo = [view(at, 1024, F16).rearrange("p (j t) -> p j t", j=8) for at in (13312, 7168)]
        turned = [view(14336 + i * 512, 512) for i in range(2)]
        roped = [view(at, 256) for at in (15360, 15616, 16640, 16896)]
        probs = sb("probs", [P, 4, PW], F32)
        masked = view(15872, 2 * PW).rearrange("p (i n) -> p i n", i=2)
        probsT = sb("probsT", [P, 4, PW], F32)
        neg_max = sb("neg_max", [P, 2, TPS], F32)
        total = sb("total", [P, 4, TPS], F32)
        inv_total = sb("inv_total", [P, 4, TPS], F32)
        rot_q = view(17408, 2 * SEQ)
        rot_k = view(17920, 2 * SEQ)
        causal = sb("causal", [P, PW], F32)
        raw_e = [view(8192 + e * 2 * F if e < 6 else 6144 + (e - 6) * 2 * F, 2 * F) for e in range(E)]
        w_hi = view(0, E * F, F16, second).rearrange("p (e k f) -> p e k f", e=E, k=2)
        w_lo = view(E * F, E * F, F16, second).rearrange("p (e k f) -> p e k f", e=E, k=2)
        hid = [view(i * 512, 512) for i in range(4)]
        hid_hi = [view(2048 + i * 512, 512, F16).rearrange("p (f t) -> p f t", f=FB) for i in range(2)]
        hid_lo = [view(3072 + i * 512, 512, F16).rearrange("p (f t) -> p f t", f=FB) for i in range(2)]
        xs_hi = [view(4096 + i * 128, 128, F16) for i in range(2)]
        xs_lo = [view(4352 + i * 128, 128, F16) for i in range(2)]
        ys = [view(4608 + i * 256, 256).rearrange("p (k d) -> p k d", d=D) for i in range(2)]
        back = [view(5120 + i * D, D) for i in range(RING * TOP)]
        xs = [view(14336 + i * 256, 256).rearrange("p (k d) -> p k d", d=D) for i in range(BODY)]

        bank = [ctx.enter_context(nc.psum_tensor(f"bank{i}", [P, 512], F32)) for i in range(8)]
        PJ, SC, TP = bank[0:3], bank[3:5], bank[5:7]
        PV = bank[7][:, 0:SEQ]
        LG = bank[6:8]
        XB, HB, YB = bank[0:2], bank[2:6], bank[6:8]

        x_in = [sem(f"x_in{i}") for i in range(NL)]
        wqk_in, wvo_in, const_in = sem("wqk_in"), sem("wvo_in"), sem("const_in")
        raw_in = [sem(f"raw_in{e}") for e in range(E)]
        raw_hi, split = sem("raw_hi"), sem("split")
        zeroed, made = sem("zeroed"), sem("made")
        dv = sem("dv")
        mean_done, squared, var_done, rstd_done, xn_done = (sem(n) for n in ("mean_done", "squared", "var_done", "rstd_done", "xn_done"))
        xT_ready, xT_hi, xT_done, logits_ready, exp_logits = (sem(n) for n in ("xT_ready", "xT_hi", "xT_done", "logits_ready", "exp_logits"))
        logits_done, mixed = sem("logits_done"), sem("mixed")
        cleared, held_ready, behind_ready, routed = (sem(n) for n in ("cleared", "held_ready", "behind_ready", "routed"))
        send_ready, sent = sem("send_ready"), sem("sent")
        pj_ready = sem("pj_ready")
        rest_hi, rest_lo = sem("rest_hi"), sem("rest_lo")
        turn_done, rope_sum, rope_hi = (sem(n) for n in ("turn_done", "rope_sum", "rope_hi"))
        q_rope_lo, k_rope_lo = sem("q_rope_lo"), sem("k_rope_lo")
        v_ready = sem("v_ready")
        q_stacked = [sem(f"q_stacked{r}") for r in range(GRP)]
        k_stacked = [sem(f"k_stacked{r}") for r in range(GRP)]
        s_ready, s_masked, exp_done, inv_done, p_ready, t_ready, pv_done = (sem(n) for n in (
            "s_ready", "s_masked", "exp_done", "inv_done", "p_ready", "t_ready", "pv_done"))
        t_out = [sem("t_out_dve"), sem("t_out_act")]
        o_hi, o_done = sem("o_hi"), sem("o_done")
        y_done = sem("y_done")
        xs_in = [sem(f"xs_in{i}") for i in range(BODY)]
        xs_ready, xs_high, xs_done = (sem(n) for n in ("xs_ready", "xs_high", "xs_done"))
        h_ready, h_gelu, h_hi, h_hi_act, h_lo, y2_ready, y2_done = (sem(n) for n in (
            "h_ready", "h_gelu", "h_hi", "h_hi_act", "h_lo", "y2_ready", "y2_done"))
        ys_out = [sem(f"ys_out{i}") for i in range(2)]
        gathered = [sem(f"gathered{i}") for i in range(RING * TOP)]
        combined, stored = sem("combined"), sem("stored")

        block = ctx.enter_context(nc.Block())

        MADE = 6
        ZEROED = 3 + E + 1 + 3
        x_tiles = x.rearrange("b (t p) d -> p (b t) d", p=P)
        out_tiles = out.rearrange("b (t p) d -> p (b t) d", p=P)

        def evicted(b, s):
            return (t_out[0], 4 * b + s // 4 + 1) if s % 4 == 0 else (t_out[1], 12 * b + s - s // 4)

        def over_samples(eng, body):
            body(0, 0, True, False)
            with eng.Fori(0, B // 2 - 1) as i:
                body(2 * i + 1, 1, False, False)
                body(2 * i + 2, 0, False, False)
            body(B - 1, 1, False, True)

        def beside(b, first, last, s):
            return [(kind, j, unit_base(b, first) + n, PJ[(n + (len(PROLOGUE) if first else 0)) % PJ_BANKS], n)
                    for n, (at, kind, j) in enumerate(units_of(first, last)) if at == s]

        def parts(which, rest, g, n=1):
            at = slice(g * SEQ, (g + n) * SEQ)
            if which == 0:
                return q_staged[:, rest, 0, at], q_staged[:, rest, 1, at]
            return k_staged[:, 0, rest, at], k_staged[:, 1, rest, at]

        def owner(kind, b):
            return b + 1 if kind in NEXT else b - 1 if kind == "y" else b

        def read_out(kind, j, of):
            return {"rest": (rest_lo, 4 * of + j + 1), "rope": (turn_done, 8 * of + j + 1), "v_low": (v_ready, 4 * of + j + 1),
                    "v_high": (v_ready, 4 * of + j + 3), "y": (y_done, 2 * of + j + 1)}[kind]

        def before(b, first, last, n):
            if n >= PJ_BANKS:
                _, kind, j = units_of(first, last)[n - PJ_BANKS]
                return read_out(kind, j, owner(kind, b))
            if first:
                return read_out(*PROLOGUE[n - PJ_BANKS], 0)
            _, kind, j = units_of(False, False)[n - PJ_BANKS]
            return read_out(kind, j, owner(kind, b - 1))

        @block.sync
        def _(sp):
            for i in range(NL):
                sp.dma_start(acc[:, i * LC:(i + 1) * LC, :], x_tiles[:, i * LC:(i + 1) * LC, :]).then_inc(x_in[i], 16)
                if i == 1:
                    sp.dma_start(raw_qk, wqk).then_inc(wqk_in, 16)
            sp.dma_start(raw_vo, wvo).then_inc(wvo_in, 16)

            pair = sorted_x.rearrange("(k p) d -> p k d", p=P)
            sp.wait_ge(zeroed, ZEROED)
            for i in range(4):
                n = ROWS // P // 4
                at, k = i * n, n if i < 3 else ROWS // P - 3 * n
                sp.dma_start(pair[:, at:at + k, :], zero_rows.unsqueeze(1).broadcast_to([P, k, D])).then_inc(cleared, 16)
            sp.dma_start(sorted_y[0:SPARE, :], zero_rows).then_inc(cleared, 16)

            def load_expert(e):
                sp.dma_start(raw_e[e], experts[:, e * 2 * F:(e + 1) * 2 * F]).then_inc(raw_in[e], 16)

            def stack_q(n, parity):
                sp.wait_ge(q_rope_lo, 4 * n + 4)
                for r in range(GRP):
                    for half_at in range(2):
                        sp.dma_start(q_stack[parity][64 * half_at:64 * half_at + 64, r, :, :].rearrange("p l n -> p (l n)"),
                                     q_staged[32 * r:32 * r + 32, :, :, :].rearrange("p k l n -> p (k l n)")).then_inc(q_stacked[r], 16)

            def stack_k(n, parity):
                sp.wait_ge(k_rope_lo, 4 * n + 4)
                for r in range(GRP):
                    for half_at in range(2):
                        sp.dma_start(k_stack[parity][64 * half_at:64 * half_at + 64, NG * r:NG * r + NG, :].rearrange("p h t -> p (h t)"),
                                     k_staged[32 * r:32 * r + 32, half_at, :, :]).then_inc(k_stacked[r], 16)

            sp.wait_ge(split, 3)
            stack_q(0, 0)
            stack_k(0, 0)

            def sample(b, parity, first, last):
                if first:
                    sp.wait_ge(routed, 1)
                    sp.wait_ge(cleared, 16 * 5)
                if not last:
                    stack_q(b + 1, 1 - parity)
                    stack_k(b + 1, 1 - parity)
                    return
                for r in range(GRP):
                    sp.wait_ge(q_stacked[r], 32 * B)
                    sp.wait_ge(k_stacked[r], 32 * B)
                for e in range(4):
                    load_expert(e)
                sp.wait_ge(y_done, TPS * (B - 1))
                for e in range(4, 6):
                    load_expert(e)

            over_samples(sp, sample)
            sp.wait_ge(y_done, TPS * B)
            for e in range(6, E):
                load_expert(e)


            def load(i, k):
                at = SPARE + i * ET
                sp.dma_start(xs[k], sorted_x[at:at + ET, :].rearrange("(k p) d -> p k d", p=P) if isinstance(i, int) else
                             sorted_x[bass.ds(at, ET), :].rearrange("(k p) d -> p k d", p=P)).then_inc(xs_in[k], 16)

            sp.wait_ge(sent, 16 * TOP * NT)
            for i in range(BODY):
                load(i, i)

            def body(n, last):
                for k in range(BODY):
                    i = BODY * n + k
                    if not last:
                        sp.wait_ge(xs_ready, i + 1)
                        load(i + BODY, k)
                    sp.wait_ge(y2_done, i + 1)
                    at = SPARE + i * ET
                    rows = sorted_y[at:at + ET, :] if isinstance(i, int) else sorted_y[bass.ds(at, ET), :]
                    sp.dma_start(rows.rearrange("(k p) d -> p k d", p=P), ys[k % 2]).then_inc(ys_out[k % 2], 16)

            with sp.Fori(0, TILES // BODY - 1) as n:
                body(n, False)
            body(TILES // BODY - 1, True)
            with sp.Fori(0, NT // 4) as c:
                sp.wait_ge(combined, 4 * TOP * c + 4 * TOP)
                sp.dma_start(out_tiles[:, bass.ds(c * 4, 4), :], acc[:, bass.ds(c * 4, 4), :]).then_inc(stored, 16)
            sp.wait_ge(stored, 16 * NT // 4)

        @block.gpsimd
        def _(pool):
            pool.dma_start(rw_f[:], rw).then_inc(const_in, 16)
            pool.dma_start(rb_all[:], rb.rearrange("(a e) -> a e", a=1).broadcast_to([P, E + 1])).then_inc(const_in, 16)
            pool.dma_start(rot_q, tables[0]).then_inc(const_in, 16)
            pool.dma_start(rot_k, tables[1]).then_inc(const_in, 16)
            nc.gpsimd.memset(ident[:], 0.0).then_inc(zeroed, 1)
            nc.gpsimd.memset(causal[:], 0.0).then_inc(zeroed, 1)
            nc.gpsimd.memset(half[:], -0.5).then_inc(zeroed, 1)
            for e in range(E + 1):
                nc.gpsimd.memset(rank[:, e:e + 1], float(E + 1 - e)).then_inc(zeroed, 1)
            nc.gpsimd.memset(below, 1.0).then_inc(zeroed, 1)
            nc.gpsimd.memset(ones, 1.0).then_inc(zeroed, 1)
            nc.gpsimd.memset(zero_rows, 0.0).then_inc(zeroed, 1)
            pool.wait_ge(zeroed, ZEROED)
            nc.gpsimd.affine_select(out=ident[:], in_=ident[:], compare_op=ALU.not_equal, fill=1.0, base=0,
                                    pattern=[[-1, P]], channel_multiplier=1).then_inc(made, 1)
            for at in (0, 2 * P):
                nc.gpsimd.affine_select(out=causal[:, at:at + P], in_=causal[:, at:at + P], compare_op=ALU.is_ge,
                                        fill=MASKED, base=0, pattern=[[-1, P]], channel_multiplier=1).then_inc(made, 1)
            nc.gpsimd.affine_select(out=below, in_=below, compare_op=ALU.is_gt, fill=0.0, base=0,
                                    pattern=[[1, P]], channel_multiplier=-1).then_inc(made, 1)
            nc.gpsimd.iota(lane_i[:], pattern=[[0, 1]], base=0, channel_multiplier=1).then_inc(made, 1)
            nc.gpsimd.iota(grid_i[:], pattern=[[1, max(PART_T)]], base=0, channel_multiplier=0).then_inc(made, 1)
            for i in range(NL):
                ts = slice(i * LC, (i + 1) * LC)
                pool.wait_ge(var_done, i + 1)
                nc.gpsimd.tensor_tensor(rstd[:, ts], small[:, 0, ts], half[:, ts], ALU.pow).then_inc(rstd_done, 1)

            def rope_add(j, m):
                if j >= 4:
                    pool.wait_ge(q_rope_lo, 4 * m + j - 3)
                elif not (isinstance(m, int) and m == 0):
                    pool.wait_ge(k_rope_lo, 4 * m + j - 3)
                pool.wait_ge(turn_done, 8 * m + j + 1)
                t = turned[j % 2]
                nc.gpsimd.tensor_tensor(roped[j % 4], t[:, 0:SEQ], t[:, SEQ:2 * SEQ], ALU.add).then_inc(rope_sum, 1)

            def q_rope_low(j, m):
                pool.wait_ge(rope_hi, 8 * m + j + 1)
                hi, lo = parts(0, 0, j)
                nc.gpsimd.tensor_tensor(lo, roped[j], hi, ALU.subtract).then_inc(q_rope_lo, 1)

            for j in range(8):
                rope_add(j, 0)
                if 1 <= j <= NG:
                    q_rope_low(j - 1, 0)

            def scale(G, s):
                pool.wait_ge(inv_done, G + 1)
                p0, p1 = probs[:, s % 4, 0:P], probs[:, s % 4, P:PW]
                nc.gpsimd.tensor_tensor(p0, p0, inv_total[:, s % 4, 0:1].broadcast_to([P, P]), ALU.mult)
                nc.gpsimd.tensor_scalar(p1, p1, inv_total[:, s % 4, 1:2], 1.0, ALU.mult, ALU.mult).then_inc(p_ready, 1)

            def send(i):
                nc.gpsimd.indirect_dma_start(
                    out=sorted_x, out_offset=bass.IndirectOffsetOnAxis(ap=send_at[:, i:i + 1], axis=0),
                    in_=send_x[:, i // TOP, :], in_offset=None).then_inc(sent, 16)

            def sample(b, parity, first, last):
                for s in range(H):
                    if not first and s in SEND_AT:
                        i = SEND_AT.index(s)
                        if i == 0:
                            pool.wait_ge(send_ready, b)
                        else:
                            pool.wait_ge(sent, 16 * (TPS * TOP * (b - 1) + i))
                    if not (first and s < INV_LAG):
                        scale(16 * b + s - INV_LAG, s - INV_LAG)
                    for kind, j, u, psum, n in beside(b, first, last, s - 3):
                        if kind == "rope" and j < NG:
                            q_rope_low(j, b + 1)
                    for kind, j, u, psum, n in beside(b, first, last, s - 1):
                        if kind == "rope":
                            rope_add(j, b + 1)
                    if not first and s in SEND_AT:
                        send(SEND_AT.index(s))

            over_samples(pool, sample)
            for lag in range(INV_LAG, 0, -1):
                scale(16 * B - lag, H - lag)

            pool.wait_ge(send_ready, B)
            for i in range(TPS * TOP):
                if i > 0:
                    pool.wait_ge(sent, 16 * (TPS * TOP * (B - 1) + i))
                send(i)

            for t in range(0, NT, 2):
                if t in (0, PARTS[0]):
                    have = PART_T[0] if t == 0 else TILES
                    for done in ys_out:
                        pool.wait_ge(done, 16 * have // 2)
                for n in range(TOP):
                    for m in range(2):
                        k = (t + m) % RING * TOP + n
                        if t >= RING:
                            pool.wait_ge(combined, (t - RING) * TOP + 2 * n + m + 1)
                        nc.gpsimd.indirect_dma_start(
                            out=back[k], out_offset=None, in_=sorted_y[0:SPARE + have * ET, :],
                            in_offset=bass.IndirectOffsetOnAxis(ap=slots[:, t + m, n:n + 1], axis=0)).then_inc(gathered[k], 16)

        @block.scalar
        def _(act):
            def raw(dst, src):
                nc.scalar.activation(dst, src, ACT.Copy, scale=W_SCALE).then_inc(raw_hi, 1)

            def square(i):
                act.wait_ge(mean_done, i + 1)
                for t in range(LC):
                    at = i * LC + t
                    last = nc.scalar.activation(xn[i % 2][:, t, :], acc[:, at, :], ACT.Square, bias=neg_mean[:, at:at + 1],
                                                accum_out=small[:, 2, at:at + 1])
                last.then_inc(squared, 1)

            def xT_high(i):
                for q in range(LQ):
                    n = i * LQ + q
                    act.wait_ge(xT_ready, n + 1)
                    nc.scalar.activation(xnT_hi[:, n * 512:(n + 1) * 512], bank[n % 4][:], ACT.Copy).then_inc(xT_hi, 1)

            for i in range(NL):
                square(i)
                if i >= 1:
                    xT_high(i - 1)
                if i == 1:
                    act.wait_ge(const_in, 64)
                    raw(rw_hi[:], rw_f[:])
                    act.wait_ge(wqk_in, 16)
                    raw(wqk_hi[:].rearrange("p g n -> p (g n)"), raw_qk)
                if i == 2:
                    act.wait_ge(wvo_in, 16)
                    raw(wvo_hi[:].rearrange("p k n -> p (k n)"), raw_vo)
            xT_high(NL - 1)

            def rest_high(j, u, psum, m, staged_before):
                if staged_before:
                    if j % 2 == 0:
                        for done in (q_stacked if j < 2 else k_stacked):
                            act.wait_ge(done, 32 * m)
                act.wait_ge(pj_ready, u + 1)
                nc.scalar.activation(parts(j // 2, 1, 2 * (j % 2), 2)[0], psum[:], ACT.Copy,
                                     scale=-UNSCALE / 8 if j < 2 else UNSCALE).then_inc(rest_hi, 1)

            def rope_high(j, m):
                act.wait_ge(rope_sum, 8 * m + j + 1)
                nc.scalar.activation(parts(j // NG, 0, j % NG)[0], roped[j % 4], ACT.Copy).then_inc(rope_hi, 1)

            def v_copy(kind, t, u, psum, done):
                if done is not None:
                    act.wait_ge(pv_done, done)
                act.wait_ge(pj_ready, u + 1)
                at = 0 if kind == "v_low" else 512
                nc.scalar.activation(v_sb[:, t, at:at + 512], psum[:], ACT.Copy, scale=UNSCALE).then_inc(v_ready, 1)

            for n, (kind, j) in enumerate(PROLOGUE):
                if kind == "rest":
                    rest_high(j, n, PJ[n % PJ_BANKS], 0, False)
                elif kind == "rope":
                    rope_high(j, 0)
                else:
                    v_copy(kind, j, n, PJ[n % PJ_BANKS], None)

            act.wait_ge(logits_done, 1)
            nc.scalar.activation(prob, logit, ACT.Exp).then_inc(exp_logits, 1)

            def t_evict(G, s):
                act.wait_ge(t_ready, G + 1)
                if not (isinstance(G, int) and G < 4):
                    act.wait_ge(pv_done, G - 3)
                nc.scalar.activation(probsT[:, s % 4, :], TP[s % 2][:, 0:PW], ACT.Copy).then_inc(t_out[1], 1)

            def o_high(G, s, parity):
                act.wait_ge(pv_done, G + 1)
                nc.scalar.activation(ot_hi[parity][:, s // 2, :], PV, ACT.Copy).then_inc(o_hi, 1)

            def split_high(e):
                act.wait_ge(raw_in[e], 16)
                nc.scalar.activation(w_hi[:, e, :, :].rearrange("p k f -> p (k f)"), raw_e[e],
                                     ACT.Copy, scale=W_SCALE).then_inc(raw_hi, 1)

            def exps(b, s, first):
                G = 16 * b + s
                act.wait_ge(s_masked, G + 1)
                if not (first and s < 4):
                    act.wait_ge(t_ready, G - 3)
                for t, (at, w) in enumerate(((0, P), (P, 2 * P))):
                    last = nc.scalar.activation(probs[:, s % 4, at:at + w], masked[:, s % 2, at:at + w], ACT.Exp,
                                                bias=neg_max[:, s % 2, t:t + 1], scale=-1.0,
                                                accum_out=total[:, s % 4, t:t + 1])
                last.then_inc(exp_done, 1)

            def sample(b, parity, first, last):
                for s in range(H):
                    for kind, j, u, psum, n in beside(b, first, last, s - 1):
                        if kind == "rest":
                            rest_high(j, u, psum, b + 1, True)
                        elif kind in ("v_low", "v_high"):
                            v_copy(kind, j, u, psum, (16 * b + 8 if kind == "v_low" else None if first else 16 * b))
                    if not (first and s < O_LAG) and (s - O_LAG) % 2 == 1:
                        o_high(16 * b + s - O_LAG, (s - O_LAG) % H, parity if s >= O_LAG else 1 - parity)
                    if not (first and s < OUT_LAG) and (s - OUT_LAG) % 4 != 0:
                        t_evict(16 * b + s - OUT_LAG, (s - OUT_LAG) % 4)
                    for kind, j, u, psum, n in beside(b, first, last, s - 2):
                        if kind == "rope":
                            rope_high(j, b + 1)
                    exps(b, s, first)
                    if last and s in (10, 11, 12, 13):
                        split_high(s - 10)

            over_samples(act, sample)
            last = (B - 1) % 2
            t_evict(16 * B - 3, 1)
            o_high(16 * B - 5, H - 5, last)
            t_evict(16 * B - 2, 2)
            t_evict(16 * B - 1, 3)
            o_high(16 * B - 3, H - 3, last)
            o_high(16 * B - 1, H - 1, last)

            act.wait_ge(y_done, TPS * B)
            for e in range(4, E):
                split_high(e)

            def xs_part(i, k):
                act.wait_ge(xs_ready, i + 1)
                if not (isinstance(i, int) and i < 2):
                    act.wait_ge(h_ready, 2 * i - 2)
                nc.scalar.activation(xs_hi[k % 2], XB[k % 2][:, 0:ET], ACT.Copy).then_inc(xs_high, 1)

            def output(i, k, first):
                act.wait_ge(y2_ready, i + 1)
                if not first:
                    act.wait_ge(ys_out[k % 2], 16 * (i // 2) if isinstance(i, int) else 8 * (i - k % 2))
                nc.scalar.activation(ys[k % 2].rearrange("p k d -> p (k d)"), YB[k % 2][:, 0:ET], ACT.Copy).then_inc(y2_done, 1)

            def body(n, first, last):
                for k in range(BODY):
                    i = BODY * n + k
                    if not (last and k == BODY - 1):
                        xs_part(i + 1, k + 1)
                    for j in range(2):
                        act.wait_ge(h_ready, 2 * i + j + 1)
                        if not (first and k < 2):
                            act.wait_ge(h_lo, 2 * i + j - 3)
                        nc.scalar.activation(hid[k % 2 * 2 + j], HB[k % 2 * 2 + j][:], ACT.Gelu, scale=UNSCALE).then_inc(h_gelu, 1)
                    act.wait_ge(h_gelu, 2 * i + 2)
                    if not (first and k < 2):
                        act.wait_ge(y2_ready, i - 1)
                    nc.scalar.activation(hid_hi[k % 2][:, 2:4, :].rearrange("p f t -> p (f t)"), hid[k % 2 * 2 + 1],
                                         ACT.Copy).then_inc(h_hi_act, 1)
                    if not (first and k == 0):
                        output(i - 1, (k - 1) % BODY, first and k <= 2)

            xs_part(0, 0)
            body(0, True, False)
            with act.Fori(1, TILES // BODY - 1) as n:
                body(n, False, False)
            body(TILES // BODY - 1, False, True)
            output(TILES - 1, BODY - 1, False)

        @block.vector
        def _(dve):
            steps = [0]

            def step(ins):
                steps[0] += 1
                ins.then_inc(dv, 1)
                dve.wait_ge(dv, steps[0])

            def low(dst, src, hi, n):
                dve.wait_ge(raw_hi, n)
                return nc.vector.scalar_tensor_tensor(dst, src, W_SCALE, hi, ALU.mult, ALU.subtract)

            def xT_low(i):
                for q in range(LQ):
                    n = i * LQ + q
                    dve.wait_ge(xT_hi, n + 1)
                    nc.vector.tensor_tensor(xnT_lo[:, n * 512:(n + 1) * 512], bank[n % 4][:],
                                            xnT_hi[:, n * 512:(n + 1) * 512], ALU.subtract).then_inc(xT_done, 1)

            def means(i):
                ts = slice(i * LC, (i + 1) * LC)
                dve.wait_ge(x_in[i], 16)
                step(nc.vector.reduce_sum(small[:, 1, ts], acc[:, ts, :], axis=AX.X))
                nc.vector.tensor_scalar(neg_mean[:, ts], small[:, 1, ts], -1.0 / D, None, ALU.mult).then_inc(mean_done, 1)

            def normalise(i):
                ts = slice(i * LC, (i + 1) * LC)
                dve.wait_ge(squared, i + 1)
                nc.vector.tensor_scalar(small[:, 0, ts], small[:, 2, ts], 1.0 / D, EPS, ALU.mult, ALU.add).then_inc(var_done, 1)
                if i >= 1:
                    xT_low(i - 1)
                dve.wait_ge(rstd_done, i + 1)
                for t in range(LC):
                    at = i * LC + t
                    last = nc.vector.tensor_scalar(xn[i % 2][:, t, :], acc[:, at, :], neg_mean[:, at:at + 1], rstd[:, at:at + 1],
                                                   ALU.add, ALU.mult)
                last.then_inc(xn_done, 1)

            means(0)
            for i in range(NL):
                if i + 1 < NL:
                    means(i + 1)
                normalise(i)
                if i == 1:
                    low(rw_lo[:], rw_f[:], rw_hi[:], 1).then_inc(split, 1)
                    low(wqk_lo[:].rearrange("p g n -> p (g n)"), raw_qk,
                        wqk_hi[:].rearrange("p g n -> p (g n)"), 2).then_inc(split, 1)
            low(wvo_lo[:].rearrange("p k n -> p (k n)"), raw_vo, wvo_hi[:].rearrange("p k n -> p (k n)"), 3).then_inc(split, 1)
            xT_low(NL - 1)

            best, key, skip = small[:, 0, :], small[:, 1, :], small[:, 3, :]

            def per_expert(v):
                return v.unsqueeze(2).broadcast_to([P, NT, E + 1])

            def router_softmax():
                dve.wait_ge(logits_ready, 1)
                bias = rb_all[:].unsqueeze(1).broadcast_to([P, NT // 2, E + 1])
                for i in range(2):
                    last = nc.vector.scalar_tensor_tensor(
                        logit[:, i * NT // 2:(i + 1) * NT // 2, :],
                        LG[i][:, 0:NT // 2 * (E + 1)].rearrange("p (t e) -> p t e", e=E + 1),
                        UNSCALE, bias, ALU.mult, ALU.add)
                step(last)
                step(nc.vector.reduce_max(best, logit, axis=AX.X))
                nc.vector.tensor_tensor(logit, logit, per_expert(best), ALU.subtract).then_inc(logits_done, 1)
                dve.wait_ge(exp_logits, 1)
                step(nc.vector.reduce_sum(best, prob, axis=AX.X))
                step(nc.vector.reciprocal(key, best))
                step(nc.vector.tensor_tensor(prob, prob, per_expert(key), ALU.mult))

            def router_choice(n, pick):
                ranks = rank[:].unsqueeze(1).broadcast_to([P, NT, E + 1])
                chosen = logit
                step(nc.vector.reduce_max(best, prob, axis=AX.X))
                step(nc.vector.tensor_tensor(pick, prob, per_expert(best), ALU.is_ge))
                step(nc.vector.tensor_tensor(pick, pick, ranks, ALU.mult))
                step(nc.vector.reduce_max(key, pick, axis=AX.X))
                step(nc.vector.tensor_tensor(pick, pick, per_expert(key), ALU.is_equal))
                step(nc.vector.tensor_tensor(chosen, pick, prob, ALU.mult))
                step(nc.vector.reduce_sum(best, chosen[:, :, 0:E], axis=AX.X))
                nc.vector.tensor_scalar(gates[:, :, n], best, UNSCALE, None, ALU.mult)
                if n == 0:
                    step(nc.vector.tensor_copy(skip, chosen[:, :, E]))
                    step(nc.vector.scalar_tensor_tensor(prob, pick, -4.0, prob, ALU.mult, ALU.add))
                else:
                    step(nc.vector.tensor_tensor(skip, skip, chosen[:, :, E], ALU.add))

            def router_slots():
                step(nc.vector.tensor_tensor(scan[0].rearrange("p (e t) -> p t e", e=E), pick0[:, :, 0:E], pick1[:, :, 0:E], ALU.add))
                src, dst = (v.rearrange("p (e t) -> p e t", e=E) for v in scan)
                d = 1
                while d < NT:
                    nc.vector.tensor_copy(dst[:, :, 0:d], src[:, :, 0:d])
                    step(nc.vector.tensor_tensor(dst[:, :, d:NT], src[:, :, d:NT], src[:, :, 0:NT - d], ALU.add))
                    src, dst = dst, src
                    d *= 2
                first = src[:, :, PARTS[0] - 1]
                nc.vector.tensor_copy(by_part(held)[:, :, 0], first)
                nc.vector.tensor_tensor(by_part(held)[:, :, 1], src[:, :, NT - 1], first, ALU.subtract).then_inc(held_ready, 1)
                dve.wait_ge(made, MADE)
                nc.vector.tensor_copy(lane, lane_i[:])
                step(nc.vector.tensor_copy(grid, grid_i[:]))
                step(nc.vector.tensor_scalar(bounds, grid[:, 0:MAX_T], float(ET), None, ALU.mult))
                dve.wait_ge(behind_ready, 1)
                step(nc.vector.tensor_copy(behind_all, bank[6][:, 0:2 * NS]))
                behind, count = behind_all[:, 0:NS], behind_all[:, NS:2 * NS]
                step(nc.vector.tensor_tensor(fills, count.unsqueeze(2).broadcast_to([P, NS, MAX_T]),
                                             bounds.unsqueeze(1).broadcast_to([P, NS, MAX_T]), ALU.is_gt))
                step(nc.vector.reduce_sum(tiles, fills, axis=AX.X))
                first_tile = by_part(start)
                step(nc.vector.memset(first_tile[:, 0, :], 0.0))
                for e in range(E):
                    step(nc.vector.tensor_tensor(first_tile[:, e + 1, :], first_tile[:, e, :], by_part(tiles)[:, e, :], ALU.add))
                step(nc.vector.scalar_tensor_tensor(by_part(base), first_tile[:, 0:E, :], float(ET), by_part(behind), ALU.mult, ALU.add))
                first_base, second_base = (by_part(base)[:, :, h] for h in range(2))
                nc.vector.tensor_scalar(first_base, first_base, float(SPARE - 1), None, ALU.add)
                step(nc.vector.scalar_tensor_tensor(second_base, second_base, float(SPARE - 1 + PART_T[0] * ET),
                                                    by_part(held)[:, :, 0], ALU.add, ALU.subtract))
                for h, ts in enumerate((slice(0, PARTS[0]), slice(PARTS[0], NT))):
                    last = nc.vector.tensor_tensor(src[:, :, ts], src[:, :, ts],
                                                   by_part(base)[:, :, h].unsqueeze(2).broadcast_to([P, E, PARTS[h]]), ALU.add)
                step(last)
                slot = src.rearrange("p e t -> p t e")
                for n, pick in enumerate((pick0, pick1)):
                    step(nc.vector.tensor_tensor(by_slot, pick[:, :, 0:E], slot, ALU.mult))
                    step(nc.vector.reduce_sum(best, by_slot, axis=AX.X))
                    step(nc.vector.scalar_tensor_tensor(best, pick[:, :, E], lane, best, ALU.mult, ALU.add))
                    step(nc.vector.tensor_copy(slots[:, :, n], best))
                step(nc.vector.memset(owner_f[0:1, :], 0.0))
                for e in range(1, E):
                    for h in range(len(PARTS)):
                        own = owner_f[0:1, h * PART_T[0]:h * PART_T[0] + PART_T[h]]
                        last = nc.vector.scalar_tensor_tensor(own, grid[0:1, 0:PART_T[h]], first_tile[0:1, e, h:h + 1], own,
                                                              ALU.is_ge, ALU.add)
                    step(last)
                own = owner_f[0:1, :].rearrange("p (n k) -> p n k", k=BODY)
                step(nc.vector.tensor_scalar(packed[0:1, :], own[:, :, 0], float(E), None, ALU.mult))
                for k in range(1, BODY):
                    step(nc.vector.scalar_tensor_tensor(packed[0:1, :], own[:, :, k], float(E ** (k + 1)), packed[0:1, :],
                                                        ALU.mult, ALU.add))
                step(nc.vector.tensor_tensor(packed[0:1, 1:], packed[0:1, 1:], own[:, 0:TILES // BODY - 1, BODY - 1], ALU.add))
                step(nc.vector.tensor_copy(body_experts[:], packed[0:1, :]))

            def router_mix():
                step(nc.vector.tensor_tensor(small[:, 0, :], skip, rstd[:], ALU.mult))
                step(nc.vector.tensor_tensor(small[:, 1, :], small[:, 0, :], neg_mean[:], ALU.mult))
                step(nc.vector.tensor_scalar(small[:, 2, :], small[:, 0, :], 1.0, None, ALU.add))
                nc.vector.tensor_copy(small[:, 3, :], small[:, 2, :]).then_inc(routed, 1)

            def dispatch(b):
                if not (isinstance(b, int) and b == 0):
                    dve.wait_ge(sent, 16 * TPS * TOP * b)
                for t in range(TPS):
                    tile = b * TPS + t
                    if isinstance(tile, int):
                        a, m, r = acc[:, tile, :], neg_mean[:, tile:tile + 1], rstd[:, tile:tile + 1]
                    else:
                        a, m, r = (v[:, bass.ds(tile, 1), :].rearrange("p a d -> p (a d)")
                                   for v in (acc, neg_mean[:].unsqueeze(2), rstd[:].unsqueeze(2)))
                    nc.vector.tensor_scalar(send_x[:, t, :], a, m, r, ALU.add, ALU.mult)
                own = slots[:, b * TPS:(b + 1) * TPS, :] if isinstance(b, int) else slots[:, bass.ds(b * TPS, TPS), :]
                nc.vector.tensor_copy(send_at[:].rearrange("p (t n) -> p t n", n=TOP), own).then_inc(send_ready, 1)

            def mix(b):
                for t in range(TPS):
                    tile = b * TPS + t
                    if isinstance(tile, int):
                        a, c1, c0 = acc[:, tile, :], small[:, 2, tile:tile + 1], small[:, 1, tile:tile + 1]
                    else:
                        a, c1, c0 = (v[:, bass.ds(tile, 1), :].rearrange("p a d -> p (a d)")
                                     for v in (acc, small[:, 2, :].unsqueeze(2), small[:, 1, :].unsqueeze(2)))
                    last = nc.vector.tensor_scalar(a, a, c1, c0, ALU.mult, ALU.add)
                last.then_inc(mixed, 1)

            def turn(j, u, psum, m):
                dve.wait_ge(pj_ready, u + 1)
                if not (isinstance(m, int) and m == 0 and j < 2):
                    dve.wait_ge(rope_sum, 8 * m + j - 1)
                nc.vector.tensor_tensor(turned[j % 2], psum[:], rot_q if j < NG else rot_k,
                                        ALU.mult).then_inc(turn_done, 1)

            def rest_low(j, psum, m):
                dve.wait_ge(rest_hi, 4 * m + j + 1)
                hi, lo = parts(j // 2, 1, 2 * (j % 2), 2)
                nc.vector.scalar_tensor_tensor(lo, psum[:], -UNSCALE / 8 if j < 2 else UNSCALE, hi,
                                               ALU.mult, ALU.subtract).then_inc(rest_lo, 1)

            def k_rope_low(j, m):
                dve.wait_ge(rope_hi, 8 * m + j + 1)
                hi, lo = parts(1, 0, j - NG)
                nc.vector.tensor_tensor(lo, roped[j % 4], hi, ALU.subtract).then_inc(k_rope_lo, 1)

            for n, (kind, j) in enumerate(PROLOGUE):
                if kind == "rest":
                    rest_low(j, PJ[n % PJ_BANKS], 0)
                elif kind == "rope":
                    turn(j, n, PJ[n % PJ_BANKS], 0)
                    if j >= NG + 2:
                        k_rope_low(j - 2, 0)
            k_rope_low(6, 0)
            k_rope_low(7, 0)
            router_softmax()
            dve.wait_ge(zeroed, ZEROED)
            router_choice(0, pick0)
            router_choice(1, pick1)
            router_slots()
            router_mix()

            def mask(b, s, first):
                G = 16 * b + s
                dve.wait_ge(s_ready, G + 1)
                if not (first and s < INV_LAG):
                    invert(G - INV_LAG, s - INV_LAG)
                for t, (at, w) in enumerate(((0, P), (P, 2 * P))):
                    last = nc.vector.tensor_tensor_reduce(
                        out=masked[:, s % 2, at:at + w], in0=SC[s % 2][:, at:at + w], in1=causal[:, at:at + w],
                        scale=1.0, scalar=MASKED, op0=ALU.add, op1=ALU.min, accum_out=neg_max[:, s % 2, t:t + 1])
                last.then_inc(s_masked, 1)

            def invert(G, s):
                dve.wait_ge(exp_done, G + 1)
                nc.vector.reciprocal(inv_total[:, s % 4, :], total[:, s % 4, :]).then_inc(inv_done, 1)

            def t_evict(G, s):
                dve.wait_ge(t_ready, G + 1)
                if not (isinstance(G, int) and G < 4):
                    dve.wait_ge(pv_done, G - 3)
                nc.vector.tensor_copy(probsT[:, s % 4, :], TP[s % 2][:, 0:PW]).then_inc(t_out[0], 1)

            def o_low(J, s, parity):
                dve.wait_ge(o_hi, J + 1)
                j = s // 2
                nc.vector.tensor_tensor(ot_lo[parity][:, j, :], PV, ot_hi[parity][:, j, :], ALU.subtract).then_inc(o_done, 1)

            def y_add(b, t, u, psum):
                dve.wait_ge(mixed, b + 1)
                dve.wait_ge(pj_ready, u + 1)
                tile = b * TPS + t
                a = acc[:, tile, :] if isinstance(tile, int) else acc[:, bass.ds(tile, 1), :].rearrange("p a d -> p (a d)")
                nc.vector.scalar_tensor_tensor(a, psum[:, 0:D], UNSCALE, a, ALU.mult, ALU.add).then_inc(y_done, 1)

            def split_low(e):
                low(w_lo[:, e, :, :].rearrange("p k f -> p (k f)"), raw_e[e],
                    w_hi[:, e, :, :].rearrange("p k f -> p (k f)"), 4 + e).then_inc(split, 1)

            def sample(b, parity, first, last):
                for s in range(H):
                    G = 16 * b + s
                    mask(b, s, first)
                    if not (first and s < OUT_LAG) and (s - OUT_LAG) % 4 == 0:
                        t_evict(G - OUT_LAG, (s - OUT_LAG) % 4)
                    for kind, j, u, psum, n in beside(b, first, last, s - 1):
                        if kind == "rope":
                            turn(j, u, psum, b + 1)
                        elif kind == "rest":
                            rest_low(j, psum, b + 1)
                        elif kind == "y":
                            y_add(b - 1, j, u, psum)
                    for kind, j, u, psum, n in beside(b, first, last, s - 3):
                        if kind == "rope" and j >= NG:
                            k_rope_low(j, b + 1)
                    if not (first and s < O_LAG) and (s - O_LAG) % 2 == 1:
                        o_low(8 * b + (s - O_LAG - 1) // 2, (s - O_LAG) % H, parity if s >= O_LAG else 1 - parity)
                    if s == 0 and not first:
                        dispatch(b - 1)
                        mix(b - 1)
                    if last and s in (11, 12, 13, 14):
                        split_low(s - 11)

            over_samples(dve, sample)
            parity = (B - 1) % 2
            invert(16 * B - 2, H - 2)
            t_evict(16 * B - 4, 0)
            invert(16 * B - 1, H - 1)
            o_low(8 * B - 3, H - 5, parity)
            o_low(8 * B - 2, H - 3, parity)
            dispatch(B - 1)
            mix(B - 1)
            o_low(8 * B - 1, H - 1, parity)
            for t in range(TPS):
                n = len(units_of(False, True)) + t
                y_add(B - 1, t, unit_base(B - 1, False) + n, PJ[n % PJ_BANKS])

            dve.wait_ge(y_done, TPS * B)
            for e in range(4, E):
                split_low(e)

            def xs_part(i, k):
                dve.wait_ge(xs_high, i + 1)
                if not (isinstance(i, int) and i < 2):
                    dve.wait_ge(h_ready, 2 * i - 2)
                nc.vector.tensor_tensor(xs_lo[k % 2], XB[k % 2][:, 0:ET], xs_hi[k % 2], ALU.subtract).then_inc(xs_done, 1)

            def hidden_parts(i, k, first):
                for j in range(2):
                    dve.wait_ge(h_gelu, 2 * i + j + 1)
                    if j == 0 and not (first and k < 2):
                        dve.wait_ge(y2_ready, i - 1)
                    h = hid[k % 2 * 2 + j]
                    hi, lo = (v[k % 2][:, 2 * j:2 * j + 2, :].rearrange("p f t -> p (f t)") for v in (hid_hi, hid_lo))
                    if j == 0:
                        nc.vector.tensor_copy(hi, h).then_inc(h_hi, 1)
                        dve.wait_ge(h_hi, i + 1)
                    else:
                        dve.wait_ge(h_hi_act, i + 1)
                    nc.vector.tensor_tensor(lo, h, hi, ALU.subtract).then_inc(h_lo, 1)

            def combine(turn, c, n):
                for m in range(2):
                    t = RING * turn + c + m
                    if isinstance(t, int):
                        a, gate = acc[:, t, :], gates[:, t, n:n + 1]
                    else:
                        a = acc[:, bass.ds(t, 1), :].rearrange("p a d -> p (a d)")
                        gate = gates[:, bass.ds(t, 1), n:n + 1].rearrange("p a d -> p (a d)")
                    at = (c + m) * TOP + n
                    dve.wait_ge(gathered[at], 16 * turn + 16)
                    if n > 0:
                        dve.wait_ge(combined, TOP * (t - m) + m + 1)
                    nc.vector.scalar_tensor_tensor(a, back[at], gate, a, ALU.mult, ALU.add).then_inc(combined, 1)

            def body(n, first, last, turn=None):
                for k in range(BODY):
                    i = BODY * n + k
                    if not (last and k == BODY - 1):
                        xs_part(i + 1, k + 1)
                    hidden_parts(i, k, first)
                    if turn is not None:
                        for c in range(sum(COMBINED[:k]), sum(COMBINED[:k + 1]), 2):
                            for m in range(TOP):
                                combine(turn, c, m)

            xs_part(0, 0)
            body(0, True, False)
            with dve.Fori(1, COMBINE_AT) as n:
                body(n, False, False)
            with dve.Fori(COMBINE_AT, TILES // BODY - 1) as n:
                body(n, False, False, n - COMBINE_AT)
            turns = TILES // BODY - COMBINE_AT
            body(TILES // BODY - 1, False, True, turns - 1)
            with dve.Fori(turns, NT // RING) as turn:
                for c in range(0, RING, 2):
                    for m in range(TOP):
                        combine(turn, c, m)
            for c in range(0, NT % RING, 2):
                for m in range(TOP):
                    combine(NT // RING, c, m)

        @block.tensor
        def _(pe):
            mm = nc.tensor.matmul

            def split3(dst, a_hi, a_lo, b_hi, b_lo, start=True, stop=True):
                mm(dst, a_hi, b_lo, start=start, stop=False)
                mm(dst, a_lo, b_hi, start=False, stop=False)
                return mm(dst, a_hi, b_hi, start=False, stop=stop)

            pe.wait_ge(made, 3)
            def logits(i):
                pe.wait_ge(xT_done, (i + 1) * LQ)
                pe.wait_ge(split, 1)
                for t in range(i * LC, (i + 1) * LC):
                    at = t % (NT // 2) * (E + 1)
                    ts = slice(t * P, (t + 1) * P)
                    last = split3(LG[t // (NT // 2)][:, at:at + E + 1], xnT_hi[:, ts], xnT_lo[:, ts], rw_hi[:], rw_lo[:])
                return last

            for i in range(NL):
                pe.wait_ge(xn_done, i + 1)
                for q in range(LQ):
                    n = i * LQ + q
                    if n >= 4:
                        pe.wait_ge(xT_done, n - 3)
                    for t in range(4):
                        last = nc.tensor.transpose(bank[n % 4][:, t * P:(t + 1) * P], xn[i % 2][:, q * 4 + t, :], ident[:])
                    last.then_inc(xT_ready, 1)
                if i >= 1:
                    logits(i - 1)
            logits(NL - 1).then_inc(logits_ready, 1)

            def unit(kind, j, b, parity, dst, free):
                if free is not None:
                    pe.wait_ge(*free)
                if kind == "y":
                    pe.wait_ge(o_done, 8 * b + 8)
                    for g in range(8):
                        last = split3(dst[:, 0:D], ot_hi[parity][:, g, j * P:(j + 1) * P], ot_lo[parity][:, g, j * P:(j + 1) * P],
                                      wo_hi[:, g, :], wo_lo[:, g, :], start=(g == 0), stop=(g == 7))
                elif kind in ("v_low", "v_high"):
                    ts = bass.ds(b * SEQ + j * P, P)
                    at = 0 if kind == "v_low" else 512
                    last = split3(dst[:], xnT_hi[:, ts], xnT_lo[:, ts], wv_hi[:, at:at + 512], wv_lo[:, at:at + 512])
                else:
                    ts = bass.ds(b * SEQ, SEQ)
                    if kind == "rope":
                        pair = (4 * (j // NG) * 2 + j % NG, 16 + j)
                    else:
                        first_g = 4 + 8 * (j // 2) + 2 * (j % 2)
                        pair = (first_g, first_g + 1)
                    for i, g in enumerate(pair):
                        last = split3(dst[:, i * SEQ:(i + 1) * SEQ], wqk_hi[:, g, :], wqk_lo[:, g, :],
                                      xnT_hi[:, ts], xnT_lo[:, ts])
                last.then_inc(pj_ready, 1)

            pe.wait_ge(split, 3)
            for n, (kind, j) in enumerate(PROLOGUE):
                unit(kind, j, 0, 0, PJ[n % PJ_BANKS], None if n < PJ_BANKS else read_out(*PROLOGUE[n - PJ_BANKS], 0))

            pe.wait_ge(made, MADE)
            pe.wait_ge(held_ready, 1)
            mm(bank[6][:, 0:NS], below, held, start=True, stop=True)
            mm(bank[6][:, NS:2 * NS], ones, held, start=True, stop=True).then_inc(behind_ready, 1)

            def scores(b, s, parity, first):
                G = 16 * b + s
                if s % GRP == 0:
                    pe.wait_ge(q_stacked[s // GRP], 32 * b + 32)
                    pe.wait_ge(k_stacked[s // GRP], 32 * b + 32)
                if not (first and s < 2):
                    pe.wait_ge(s_masked, G - 1)
                for at, w in ((0, P), (P, 2 * P)):
                    qs = slice(0, P) if at == 0 else slice(P, 2 * P)
                    dst = SC[s % 2][:, at:at + w]
                    q_lo, q_hi = (q_stack[parity][:, s // NG, l, s % NG * SEQ + qs.start:s % NG * SEQ + qs.stop] for l in (1, 0))
                    mm(dst, q_lo, k_stack[parity][:, s, 0:w], start=True, stop=False)
                    last = mm(dst, q_hi, k_stack[parity][:, s, 0:w], start=False, stop=True)
                last.then_inc(s_ready, 1)

            def transposes(G, s, free):
                pe.wait_ge(p_ready, G + 1)
                if free is not None:
                    pe.wait_ge(*free)
                for k in range(3):
                    last = nc.tensor.transpose(TP[s % 2][:, k * P:(k + 1) * P], probs[:, s % 4, k * P:(k + 1) * P], ident[:])
                last.then_inc(t_ready, 1)

            def attend(b, j, first):
                if j % 4 == 0:
                    pe.wait_ge(v_ready, 4 * b + (2 if j == 0 else 4))
                if not (first and j < 1):
                    pe.wait_ge(o_done, 8 * b + j)
                for i in range(2):
                    s = 2 * j + i
                    pe.wait_ge(*evicted(b, s))
                    rows = slice(64 * i, 64 * i + 64)
                    vs = slice(s * DK, (s + 1) * DK)
                    mm(PV[rows, :], v_sb[:, 0, vs], probsT[:, s % 4, 0:SEQ], start=True, stop=False)
                    mm(PV[rows, P:SEQ], v_sb[:, 1, vs], probsT[:, s % 4, SEQ:PW], start=False, stop=True).then_inc(pv_done, 1)

            def sample(b, parity, first, last):
                for s in range(H):
                    G = 16 * b + s
                    scores(b, s, parity, first)
                    for kind, j, u, psum, n in beside(b, first, last, s):
                        unit(kind, j, owner(kind, b), parity if kind == "v_high" else 1 - parity, psum, before(b, first, last, n))
                    if not (first and s < T_LAG):
                        transposes(G - T_LAG, (s - T_LAG) % 4, None if first and s < T_LAG + 2 else
                                   evicted(b, s - T_LAG - 2) if s >= T_LAG + 2 else evicted(b - 1, s - T_LAG - 2 + H))
                    if (s - PV_LAG) % 2 == 1:
                        if s > PV_LAG:
                            attend(b, (s - PV_LAG) // 2, first)
                        elif not first:
                            attend(b - 1, (s - PV_LAG + H) // 2, False)

            over_samples(pe, sample)
            for s in range(H, H + PV_LAG):
                if s < H + T_LAG:
                    transposes(16 * (B - 1) + s - T_LAG, (s - T_LAG) % 4, evicted(B - 1, s - T_LAG - 2))
                if (s - PV_LAG) % 2 == 1:
                    attend(B - 1, (s - PV_LAG) // 2, False)
            for t in range(TPS):
                n = len(units_of(False, True)) + t
                unit("y", t, B - 1, (B - 1) % 2, PJ[n % PJ_BANKS], before(B - 1, False, True, n))

            def tokens(i, k):
                if not (isinstance(i, int) and i < 2):
                    pe.wait_ge(xs_done, i - 1)
                pe.wait_ge(xs_in[k % BODY], 4 * (i - k % BODY) + 16)
                for j in range(ET // P):
                    last = nc.tensor.transpose(XB[k % 2][:, j * P:(j + 1) * P], xs[k % BODY][:, j, :], ident[:])
                last.then_inc(xs_ready, 1)

            def expert_weights(w, e, which, at):
                return w[:, bass.ds(e, 1), which, at].rearrange("p a n -> p (a n)")

            def hidden(e, k):
                for j in range(2):
                    for f in range(2):
                        fs = slice((2 * j + f) * P, (2 * j + f + 1) * P)
                        last = split3(HB[k % 2 * 2 + j][:, f * ET:(f + 1) * ET], expert_weights(w_hi, e, 0, fs),
                                      expert_weights(w_lo, e, 0, fs), xs_hi[k % 2], xs_lo[k % 2])
                    last.then_inc(h_ready, 1)

            def down(i, e, k, first):
                pe.wait_ge(h_lo, 2 * i + 2)
                if not first:
                    pe.wait_ge(y2_done, i - 1)
                for j in range(ET // P):
                    ts = slice(j * P, (j + 1) * P)
                    for fb in range(FB):
                        ds = slice(fb * D, (fb + 1) * D)
                        last = split3(YB[k % 2][:, ts], hid_hi[k % 2][:, fb, ts], hid_lo[k % 2][:, fb, ts],
                                      expert_weights(w_hi, e, 1, ds), expert_weights(w_lo, e, 1, ds),
                                      start=(fb == 0), stop=(fb == FB - 1))
                last.then_inc(y2_ready, 1)

            def two_bodies(n, first, last):
                words = body_experts[:].bitcast(I32)
                packed = pe.value_load(words[0:1, n:n + 1] if isinstance(n, int) else words[0:1, bass.ds(n, 1)],
                                       min_val=0, max_val=2 ** 31 - 1)
                for half in range(2):
                    e = [(packed >> (16 * half + BITS * k)) & (E - 1) for k in range(BODY + 1)]
                    for k in range(BODY):
                        i = 2 * BODY * n + half * BODY + k
                        start, end = first and half == 0, last and half == 1
                        pe.wait_ge(xs_done, i + 1)
                        if not (start and k < 2):
                            pe.wait_ge(h_gelu, 2 * i - 2)
                        if not (end and k == BODY - 1):
                            tokens(i + 1, k + 1)
                        hidden(e[k + 1], k)
                        if not (start and k == 0):
                            down(i - 1, e[k], k - 1, start and k <= 2)
                return e[BODY]

            pe.wait_ge(y_done, TPS * B)
            pe.wait_ge(split, 3 + E)
            tokens(0, 0)
            two_bodies(0, True, False)
            with pe.Fori(1, TILES // BODY // 2 - 1) as n:
                two_bodies(n, False, False)
            e = two_bodies(TILES // BODY // 2 - 1, False, True)
            down(TILES - 1, e, BODY - 1, False)


def rotation_tables(np):
    inv = (1.0 / np.power(np.float32(6000.0), np.arange(0, ROPE, 2, dtype=np.float32) / np.float32(ROPE))).astype(np.float32)
    angle = np.outer(np.arange(SEQ, dtype=np.float32), inv).astype(np.float32)
    angle = np.concatenate([angle, angle], axis=1).T.astype(np.float64)
    sign = np.where(np.arange(ROPE) < ROPE // 2, -1.0, 1.0)[:, None]
    one = np.concatenate([np.cos(angle).astype(np.float32), (sign * np.sin(angle)).astype(np.float32)], axis=1)
    one = np.tile(one, (GRP, 1))
    return np.stack([one * np.float32(-UNSCALE / 8), one * np.float32(UNSCALE)]).astype(np.float32)


def kernel(**inputs):
    import numpy as np
    import concourse.bacc as bacc
    from concourse.bass_utils import run_bass_kernel_spmd

    wqkv, wo = np.asarray(inputs["L0_attn_W_qkv"]), np.asarray(inputs["L0_attn_W_o"])
    order = [GRP * g + r for r in range(GRP) for g in range(NG)]
    swap = list(range(ROPE // 2, ROPE)) + list(range(ROPE // 2))
    groups = []
    for which in (0, 1):
        for part in (slice(0, ROPE), slice(ROPE, DK)):
            groups += [wqkv[which, GRP * g:GRP * g + GRP, part].reshape(P, D) for g in range(NG)]
    for which in (0, 1):
        groups += [wqkv[which, GRP * g:GRP * g + GRP][:, swap].reshape(P, D) for g in range(NG)]
    arrays = {
        "x": np.ascontiguousarray(inputs["L0_attn_x"]),
        "wqk": np.ascontiguousarray(np.concatenate(groups).T),
        "wvo": np.ascontiguousarray(np.concatenate([
            wqkv[2][order].reshape(H * DK, D).T,
            wo.reshape(D, H, DK)[:, order].reshape(D, 8, P).transpose(2, 1, 0).reshape(P, 8 * D)], axis=1)),
        "rw": np.ascontiguousarray(inputs["L0_ffn_router_w"]),
        "rb": np.ascontiguousarray(inputs["L0_ffn_router_b"]),
        "experts": np.ascontiguousarray(np.concatenate([
            np.asarray(inputs["L0_ffn_w1"]).transpose(1, 0, 2),
            np.asarray(inputs["L0_ffn_w2"]).reshape(E, FB, P, D).transpose(2, 0, 1, 3).reshape(P, E, FB * D)], axis=2).reshape(P, E * 2 * F)),
        "tables": rotation_tables(np),
    }
    nc = bacc.Bacc("TRN2", target_bir_lowering=False, num_devices=1)
    args = [nc.dram_tensor(f"{n}_dram", a.shape, F32, kind="ExternalInput").ap() for n, a in arrays.items()]
    out = nc.dram_tensor("out_dram", (B, SEQ, D), F32, kind="ExternalOutput").ap()
    sorted_x, sorted_y = (nc.dram_tensor(n, (ROWS, D), F32, kind="Internal").ap() for n in ("sorted_x_dram", "sorted_y_dram"))
    attention_and_experts(nc, *args, sorted_x, sorted_y, out)
    r = run_bass_kernel_spmd(nc, [{f"{n}_dram": a for n, a in arrays.items()}], core_ids=[0])
    return r.results[0]["out_dram"]
```
